# Optimizing a Trainium2 kernel written in Bass

```python
import numpy as np
import jax
import jax.numpy as jnp

def _softmax(x, axis=-1):
    return jax.nn.softmax(x, axis=axis)

def _gelu(x):
    return jax.nn.gelu(x, approximate=True)

def _silu(x):
    return jax.nn.silu(x)

def _sigmoid(x):
    return jax.nn.sigmoid(x)

def _layernorm(x, axis=-1, eps=1e-05):
    m = jnp.mean(x, axis=axis, keepdims=True)
    v = jnp.var(x, axis=axis, keepdims=True)
    return (x - m) / jnp.sqrt(v + eps)

def _scatter_add(tgt, idx, src, axis=0):
    return tgt.at[idx].add(src)

def _segment_sum(src, seg, n):
    return jax.ops.segment_sum(src, seg, n)
kernel_name = 'mk_adj_preln_d4_adj_r2_74a033'

def setup_inputs(seed: int=0):
    np.random.seed(seed)
    _w = jnp.asarray

    def _rec_inputs():
        import jax
        import jax.numpy as jnp
        _gk = jax.random.key(seed)
        x = -0.0003929 + 0.9999 * jax.random.normal(jax.random.fold_in(_gk, 1), (16, 512, 256), jnp.float32)
        _a = jax.random.bernoulli(jax.random.fold_in(_gk, 2), 0.015625, (16, 512, 512))
        _a = jnp.logical_or(_a, jnp.eye(512, dtype=bool))
        _af = _a.astype(jnp.float32)
        _af = _af * jax.random.uniform(jax.random.fold_in(_gk, 3), (16, 512, 512), jnp.float32, 0.05, 1)
        adj = _af
        return (x, adj)
    x, adj = _rec_inputs()

    def _L0_gnn_setup():
        import jax, jax.numpy as jnp
        import numpy as np
        EPS = 1e-06
        key = jax.random.key(seed)
        k1, k2, k3 = jax.random.split(key, 3)
        B, N, F, O = (8, 2048, 256, 256)
        x = jax.random.normal(k1, (B, N, F), dtype=jnp.float32)
        adj = jax.random.uniform(k2, (B, N, N), dtype=jnp.float32)
        W = jax.random.normal(k3, (O, 2 * F), dtype=jnp.float32) * (1.0 / np.sqrt(2 * F))
        return {'x': x, 'adj': adj, 'W': W}
    _L0_gnn_all = _L0_gnn_setup()
    _L0_gnn_in = {k: v for k, v in _L0_gnn_all.items() if k in ('W',)}
    del _L0_gnn_all

    def _L1_gnn_setup():
        import jax, jax.numpy as jnp
        import numpy as np
        EPS_LN = 1e-05

        def hypergraph_conv(x, adj, W, b):
            N, C, _ = adj.shape
            H = (adj != 0).astype(x.dtype)
            w = adj.reshape(N, -1)[:, :C]
            xw = jnp.einsum('ncd,hd->nch', x, W)
            Dn = jnp.einsum('nce,ne->nc', H, w)
            Dn = jnp.where(Dn > 0, 1.0 / Dn, 0.0)
            Be = H.sum(axis=1)
            Be = jnp.where(Be > 0, 1.0 / Be, 0.0)
            m = Be[:, :, None] * jnp.einsum('nce,nch->neh', H, xw)
            out = Dn[:, :, None] * jnp.einsum('nce,neh->nch', H, m)
            return out + b

        def layer_norm(x, g, b):
            mu = jnp.mean(x, axis=-1, keepdims=True)
            var = jnp.var(x, axis=-1, keepdims=True)
            return (x - mu) * jax.lax.rsqrt(var + EPS_LN) * g + b
        key = jax.random.key(seed)
        ks = jax.random.split(key, 4)
        N, C, Din, Dh, Dout = (16, 512, 256, 512, 256)
        x = jax.random.normal(ks[0], (N, C, Din), dtype=jnp.float32)
        adj = jax.random.uniform(ks[1], (N, C, C), dtype=jnp.float32, minval=0.1, maxval=1.0)
        W1 = jax.random.normal(ks[2], (Dh, Din), dtype=jnp.float32) * (1.0 / np.sqrt(Din))
        b1 = jnp.zeros((Dh,), dtype=jnp.float32)
        gamma = jnp.ones((Dh,), dtype=jnp.float32)
        beta = jnp.zeros((Dh,), dtype=jnp.float32)
        W2 = jax.random.normal(ks[3], (Dout, Dh), dtype=jnp.float32) * (1.0 / np.sqrt(Dh))
        b2 = jnp.zeros((Dout,), dtype=jnp.float32)
        return {'x': x, 'adj': adj, 'W1': W1, 'b1': b1, 'gamma': gamma, 'beta': beta, 'W2': W2, 'b2': b2}
    _L1_gnn_all = _L1_gnn_setup()
    _L1_gnn_in = {k: v for k, v in _L1_gnn_all.items() if k in ('W1', 'b1', 'gamma', 'beta', 'W2', 'b2')}
    del _L1_gnn_all

    def _L2_gnn_setup():
        import jax, jax.numpy as jnp
        import numpy as np
        EMBED_DIM = 256
        NUM_HEADS = 8
        HEAD_DIM = EMBED_DIM // NUM_HEADS
        SCALE = HEAD_DIM ** (-0.5)
        B, S = (16, 512)
        key = jax.random.key(seed)
        ks = jax.random.split(key, 12)
        init = lambda k, shape: jax.random.normal(k, shape, dtype=jnp.float32) * EMBED_DIM ** (-0.5)
        return {'x': jax.random.normal(ks[0], (B, S, EMBED_DIM), dtype=jnp.float32), 'adj_matrix': jax.random.uniform(ks[1], (B, S, S), dtype=jnp.float32), 'bond_matrix': jax.random.uniform(ks[2], (B, S, S), dtype=jnp.float32), 'Wq': init(ks[3], (EMBED_DIM, EMBED_DIM)), 'bq': jnp.zeros((EMBED_DIM,), jnp.float32), 'Wk': init(ks[4], (EMBED_DIM, EMBED_DIM)), 'bk': jnp.zeros((EMBED_DIM,), jnp.float32), 'Wv': init(ks[5], (EMBED_DIM, EMBED_DIM)), 'bv': jnp.zeros((EMBED_DIM,), jnp.float32), 'Wo': init(ks[6], (EMBED_DIM, EMBED_DIM)), 'bo': jnp.zeros((EMBED_DIM,), jnp.float32), 'seq_len': S}
    _L2_gnn_all = _L2_gnn_setup()
    _L2_gnn_in = {k: v for k, v in _L2_gnn_all.items() if k in ('Wq', 'bq', 'Wk', 'bk', 'Wv', 'bv', 'Wo', 'bo')}
    del _L2_gnn_all

    def _L3_gnn_setup():
        import jax, jax.numpy as jnp
        import numpy as np
        B, N, DIN, DOUT = (8, 1024, 256, 256)
        EDGE_P = 0.01

        def _gcn_norm(adj):
            A = (adj != 0).astype(adj.dtype)
            eye = jnp.eye(A.shape[-1], dtype=A.dtype)
            A = jnp.maximum(A, eye)
            deg = A.sum(axis=-1)
            dinv = jnp.where(deg > 0, jax.lax.rsqrt(deg), 0.0)
            return dinv[..., :, None] * A * dinv[..., None, :]
        key = jax.random.key(seed)
        k1, k2, k3, k4 = jax.random.split(key, 4)
        inputs = jax.random.normal(k1, (B, N, DIN), dtype=jnp.float32)
        adj = (jax.random.uniform(k2, (B, N, N)) < EDGE_P).astype(jnp.float32)
        W = jax.random.normal(k3, (DIN, DOUT), dtype=jnp.float32) / np.sqrt(DIN)
        b = jax.random.normal(k4, (DOUT,), dtype=jnp.float32) * 0.01
        return {'inputs': inputs, 'adj': adj, 'W': W, 'b': b}
    _L3_gnn_all = _L3_gnn_setup()
    _L3_gnn_in = {k: v for k, v in _L3_gnn_all.items() if k in ('W', 'b')}
    del _L3_gnn_all
    return {'x': x, 'adj': adj, 'L0_gnn_W': _L0_gnn_in['W'], 'L1_gnn_W1': _L1_gnn_in['W1'], 'L1_gnn_b1': _L1_gnn_in['b1'], 'L1_gnn_gamma': _L1_gnn_in['gamma'], 'L1_gnn_beta': _L1_gnn_in['beta'], 'L1_gnn_W2': _L1_gnn_in['W2'], 'L1_gnn_b2': _L1_gnn_in['b2'], 'L2_gnn_Wq': _L2_gnn_in['Wq'], 'L2_gnn_bq': _L2_gnn_in['bq'], 'L2_gnn_Wk': _L2_gnn_in['Wk'], 'L2_gnn_bk': _L2_gnn_in['bk'], 'L2_gnn_Wv': _L2_gnn_in['Wv'], 'L2_gnn_bv': _L2_gnn_in['bv'], 'L2_gnn_Wo': _L2_gnn_in['Wo'], 'L2_gnn_bo': _L2_gnn_in['bo'], 'L3_gnn_W': _L3_gnn_in['W'], 'L3_gnn_b': _L3_gnn_in['b']}

def reference(x, adj, L0_gnn_W, L1_gnn_W1, L1_gnn_b1, L1_gnn_gamma, L1_gnn_beta, L1_gnn_W2, L1_gnn_b2, L2_gnn_Wq, L2_gnn_bq, L2_gnn_Wk, L2_gnn_bk, L2_gnn_Wv, L2_gnn_bv, L2_gnn_Wo, L2_gnn_bo, L3_gnn_W, L3_gnn_b):
    import jax
    import jax.numpy as jnp

    def _L0_gnn_ref(x, adj, W):
        import jax, jax.numpy as jnp
        import numpy as np
        EPS = 1e-06
        deg = jnp.sum(adj, axis=-1, keepdims=True)
        agg = jnp.einsum('bij,bjf->bif', adj, x) / jnp.maximum(deg, EPS)
        cat = jnp.concatenate([x, agg], axis=2)
        out = jnp.einsum('bnf,of->bno', cat, W)
        return jax.nn.relu(out)

    def _L1_gnn_ref(x, adj, W1, b1, gamma, beta, W2, b2):
        import jax, jax.numpy as jnp
        import numpy as np
        EPS_LN = 1e-05

        def hypergraph_conv(x, adj, W, b):
            N, C, _ = adj.shape
            H = (adj != 0).astype(x.dtype)
            w = adj.reshape(N, -1)[:, :C]
            xw = jnp.einsum('ncd,hd->nch', x, W)
            Dn = jnp.einsum('nce,ne->nc', H, w)
            Dn = jnp.where(Dn > 0, 1.0 / Dn, 0.0)
            Be = H.sum(axis=1)
            Be = jnp.where(Be > 0, 1.0 / Be, 0.0)
            m = Be[:, :, None] * jnp.einsum('nce,nch->neh', H, xw)
            out = Dn[:, :, None] * jnp.einsum('nce,neh->nch', H, m)
            return out + b

        def layer_norm(x, g, b):
            mu = jnp.mean(x, axis=-1, keepdims=True)
            var = jnp.var(x, axis=-1, keepdims=True)
            return (x - mu) * jax.lax.rsqrt(var + EPS_LN) * g + b
        h = jax.nn.relu(hypergraph_conv(x, adj, W1, b1))
        h = layer_norm(h, gamma, beta)
        y = hypergraph_conv(h, adj, W2, b2)
        return y + x

    def _L2_gnn_ref(x, adj_matrix, bond_matrix, Wq, bq, Wk, bk, Wv, bv, Wo, bo, seq_len):
        import jax, jax.numpy as jnp
        import numpy as np
        EMBED_DIM = 256
        NUM_HEADS = 8
        HEAD_DIM = EMBED_DIM // NUM_HEADS
        SCALE = HEAD_DIM ** (-0.5)
        B, S = (16, 512)
        b = x.shape[0]

        def proj(W, bias):
            y = jnp.einsum('bse,fe->bsf', x, W) + bias
            return y.reshape(b, seq_len, NUM_HEADS, HEAD_DIM).transpose(0, 2, 1, 3)
        q, k, v = (proj(Wq, bq), proj(Wk, bk), proj(Wv, bv))
        scores = jnp.einsum('bhqd,bhkd->bhqk', q, k) * SCALE
        mask = (adj_matrix + bond_matrix)[:, None, :, :]
        scores = scores * mask
        attn = jax.nn.softmax(scores, axis=-1)
        ctx = jnp.einsum('bhqk,bhkd->bhqd', attn, v)
        ctx = ctx.transpose(0, 2, 1, 3).reshape(b, seq_len, EMBED_DIM)
        return jnp.einsum('bse,fe->bsf', ctx, Wo) + bo

    def _L3_gnn_ref(inputs, adj, W, b):
        import jax, jax.numpy as jnp
        import numpy as np
        B, N, DIN, DOUT = (8, 1024, 256, 256)
        EDGE_P = 0.01

        def _gcn_norm(adj):
            A = (adj != 0).astype(adj.dtype)
            eye = jnp.eye(A.shape[-1], dtype=A.dtype)
            A = jnp.maximum(A, eye)
            deg = A.sum(axis=-1)
            dinv = jnp.where(deg > 0, jax.lax.rsqrt(deg), 0.0)
            return dinv[..., :, None] * A * dinv[..., None, :]
        norm = _gcn_norm(adj)
        h = jnp.einsum('bnf,fo->bno', inputs, W)
        agg = jnp.einsum('bnm,bmo->bno', norm, h)
        return jnp.tanh(agg + b)
    h = jnp.maximum(_layernorm(x, axis=-1), 0.0)
    x = x + _L0_gnn_ref(h, adj, L0_gnn_W)
    h = jnp.maximum(_layernorm(x, axis=-1), 0.0)
    x = x + _L1_gnn_ref(h, adj, L1_gnn_W1, L1_gnn_b1, L1_gnn_gamma, L1_gnn_beta, L1_gnn_W2, L1_gnn_b2)
    h = jnp.maximum(_layernorm(x, axis=-1), 0.0)
    x = x + _L2_gnn_ref(h, adj, adj, L2_gnn_Wq, L2_gnn_bq, L2_gnn_Wk, L2_gnn_bk, L2_gnn_Wv, L2_gnn_bv, L2_gnn_Wo, L2_gnn_bo, 512)
    h = jnp.maximum(_layernorm(x, axis=-1), 0.0)
    x = x + _L3_gnn_ref(h, adj, L3_gnn_W, L3_gnn_b)
    return x

_drawn_inputs = setup_inputs


def setup_inputs(seed=0):
    import zlib

    import numpy as np

    out = dict(_drawn_inputs(seed))
    spreads = {'L1_gnn_b1': (0.0, 0.1),
     'L1_gnn_gamma': (1.0, 0.2),
     'L1_gnn_beta': (0.0, 0.1),
     'L1_gnn_b2': (0.0, 0.8),
     'L2_gnn_bq': (0.0, 2.0),
     'L2_gnn_bk': (0.0, 2.0),
     'L2_gnn_bv': (0.0, 0.792),
     'L2_gnn_bo': (0.0, 0.8)}
    factors = {'L2_gnn_Wq': 8.0, 'L2_gnn_Wk': 8.0, 'L3_gnn_b': 64.0}
    for name, (base, spread) in spreads.items():
        noise = np.random.default_rng([zlib.crc32(name.encode()), seed]).standard_normal(out[name].shape)
        drawn = base * np.exp(spread * noise) if base else spread * noise
        out[name] = jnp.asarray(drawn.astype(out[name].dtype))
    for name, factor in factors.items():
        out[name] = (out[name] * factor).astype(out[name].dtype)
    return out
```

```python
from contextlib import ExitStack

import concourse.bass as bass
from concourse import mybir

F32 = mybir.dt.float32
F32R = mybir.dt.float32r
F16 = mybir.dt.float16
BF16 = mybir.dt.bfloat16
ALU = mybir.AluOpType
ACT = mybir.ActivationFunctionType
AX_X = mybir.AxisListType.X

P = 128
DMA = 16
CONSTS = 5
LN_EPS = 1e-5
DEG_EPS = 1e-6
TINY = 1e-38
PROB_SCALE = 1024.0


class Signal:

    def __init__(self, semaphore, per_batch):
        self.semaphore, self.per_batch = semaphore, per_batch

    def after(self, b, n):
        return b * self.per_batch + n


def wait(eng, signal, b, n):
    eng.wait_ge(signal.semaphore, signal.after(b, n))


def wait_for_earlier_batches(eng, signal, b):
    if isinstance(b, int) and b == 0:
        return
    eng.wait_ge(signal.semaphore, signal.after(b, 0))


class Bank:

    def __init__(self, tiles, filled, drained):
        self.tiles, self.filled, self.drained = tiles, filled, drained

    def tile(self, u):
        return self.tiles[u % 2]

    def wait_free(self, eng, b, u):
        s = self.drained[u % 2]
        n = s.after(b, u // 2)
        if not (isinstance(n, int) and n == 0):
            eng.wait_ge(s.semaphore, n)

    def wait_read_out(self, eng, b, inputs, u):
        for k in range(2):
            uses = [v for v in (*inputs, u - 2) if v % 2 == k]
            if uses:
                self.wait_drained(eng, b, max(uses))

    def wait_filled(self, eng, b, u):
        eng.wait_ge(self.filled[u % 2].semaphore, self.filled[u % 2].after(b, u // 2 + 1))

    def wait_drained(self, eng, b, u):
        eng.wait_ge(self.drained[u % 2].semaphore, self.drained[u % 2].after(b, u // 2 + 1))

    def fill(self, instruction, u):
        instruction.then_inc(self.filled[u % 2].semaphore, 1)

    def drain(self, instruction, u):
        instruction.then_inc(self.drained[u % 2].semaphore, 1)


FRONT = (
    [("norm0", 0), ("turn0", 0), ("turn0", 1)]
    + [("project0", t) for t in range(4)]
    + [s for t in range(4) for s in (("masks", t), ("aggregate0", t))]
    + [("norm1", 0), ("split1", 0)]
    + [("edges1", g) for g in range(2)]
    + [("nodes1", t) for t in range(2)]
    + [("expand1", t) for t in range(4)]
    + [("norm_r", 0)]
    + [("turn1", t) for t in range(4)]
    + [("contract1", g) for g in range(2)]
    + [("split2", 0)]
    + [("edges2", g) for g in range(2)]
    + [("nodes2", g) for g in range(2)]
)
HEAD = [
    ("late", "norm3", 0), ("back", "norm2", 0),
    ("late", "turn3", 0), ("late", "turn3", 1), ("back", "turn2", 0), ("back", "turn2", 1),
    ("late", "project3", 0), ("late", "project3", 1), ("back", "queries", 0), ("back", "queries", 1),
    ("late", "aggregate3", 0), ("late", "aggregate3", 1), ("back", "keep", 0),
    ("back", "keys", 0), ("back", "keys", 1), ("back", "values", 0), ("back", "values", 1), ("back", "value_parts", 0),
]
TAIL = [("back", "turn_ctx", 0), ("back", "turn_ctx", 1), ("back", "output2", 0), ("back", "output2", 1)]
GROUPS = {"late": -1, "back": 0, "front": 1}
NT = 32

PACE = {
    "tensor": [("context", -3), ("probs", -1), ("scores", 1)],
    "vector": [("scores", 0), ("probs", -2), ("weigh", -3)],
    "scalar": [("scores", 0), ("probs", -1)],
    "gpsimd": [],
}
BEFORE, AFTER = 1, 3

FRONT_SLOT = {
    "tensor": [
        0, 2, 3, 6, 8, 11, 11, 14, 18, 19, 21, 23, 24, 25, 26, 27, 29, 31, 32, 34, 34, 35, 36, 38, 39, 40,
        44, 45, 46, 48, 50, 50, 53, 54, 55, 57, 57],
    "vector": [
        0, 2, 3, 6, 8, 10, 11, 14, 19, 20, 22, 24, 25, 26, 27, 28, 30, 32, 33, 34, 35, 36, 37, 39, 40, 41,
        45, 46, 47, 49, 50, 51, 54, 55, 57, 57, 57],
    "scalar": [
        0, 2, 3, 6, 8, 10, 11, 14, 18, 19, 21, 23, 24, 25, 26, 27, 29, 31, 32, 33, 34, 36, 37, 40, 40, 40,
        44, 45, 46, 48, 49, 50, 53, 54, 55, 57, 57],
    "gpsimd": [
        0, 2, 3, 6, 8, 10, 11, 14, 18, 19, 21, 23, 24, 25, 26, 27, 29, 31, 32, 33, 34, 35, 36, 38, 39, 40,
        44, 45, 46, 48, 49, 50, 53, 54, 55, 57, 57],
}


def attention_step(t, pace):
    step = []
    for stage, ahead in pace:
        u = t + ahead
        if 0 <= u < NT and stage != "weigh":
            step.append(("back", stage, u))
        if 0 <= u < NT and stage == "weigh" and u % 4 == 3:
            step.append(("back", stage, u // 4))
    return step


def body(engine, groups):
    slots = ([[s] for s in HEAD]
             + [attention_step(t, PACE[engine]) for t in range(-BEFORE, NT + AFTER)]
             + [[s] for s in TAIL])
    order, done = [], 0
    for i, slot in enumerate(slots):
        order += slot
        while done < len(FRONT) and (FRONT_SLOT[engine][done] <= i or i == len(slots) - 1):
            order.append(("front", *FRONT[done]))
            done += 1
    return [s for s in order if s[0] in groups]


F_TURN0, F_PROJECT0, F_AGG0, F_EDGES1, F_NODES1, F_EXPAND1, F_TURN1, F_CONTRACT1, F_EDGES2, F_NODES2 = (
    0, 2, 6, 10, 12, 14, 18, 22, 24, 26)
F_USES = 28
B_TURN2, B_QUERIES, B_KEYS, B_VALUES, B_SCORES = 0, 2, 4, 6, 8
B_USES = B_SCORES + NT
T_PROBS, T_TURN_CTX, T_OUTPUT2, T_TURN3, T_PROJECT3, T_AGG3 = 0, NT, NT + 2, NT + 4, NT + 6, NT + 8
T_USES = NT + 10


def gnn_stack(nc, x, adj, adjT, w0T, w1T, b1, gamma_cols, beta_cols, w2T, b2, wqT, bq_cols, wkT, bk_cols, wvT, bv, woT, bo,
              w3, b3, out):
    B, N, D = x.shape
    NTILE = N // P
    DT = D // P
    DH = w1T.shape[1]
    HT = DH // P
    HEADS = 8
    HD = D // HEADS
    PER_TILE = P // HD
    PARTS = 3
    SCORE_SCALE = 2.0 * HD ** -0.5
    assert N == 512 and D == 256 and DH == 512 and NT == NTILE * HEADS

    with ExitStack() as ctx:
        def sb(name, shape, dt=F32):
            return ctx.enter_context(nc.sbuf_tensor(name, shape, dt))

        def sem(name):
            return ctx.enter_context(nc.semaphore(name))

        def signal(name, per_batch=1):
            return Signal(sem(name), per_batch)

        def banks(name, uses):
            tiles = [ctx.enter_context(nc.psum_tensor(f"{name}{i}", [P, 512], F32)) for i in range(2)]
            return Bank(tiles, [signal(f"{name}_filled{i}", uses // 2) for i in range(2)],
                        [signal(f"{name}_drained{i}", uses // 2) for i in range(2)])

        front = banks("front", F_USES)
        back = banks("back", B_USES)
        turned = banks("turned", T_USES)
        mixed = banks("mixed", 8)

        ident = sb("ident", [P, P])
        eps4 = sb("eps4", [P, NTILE])
        minus1 = sb("minus1", [P, NTILE])
        minus_half = sb("minus_half", [P, NTILE])
        WIDTH = dict(w0=(DT, 2 * D), w1=(DT, DH), w2=(HT, D), wq=(DT, D), wk=(DT, D), wv=(DT, D), wo=(DT, D),
                     w3=(DT, D))
        w_hi = {n: sb(f"{n}_hi", [P, *s], F32R) for n, s in WIDTH.items()}
        w_lo = {n: sb(f"{n}_lo", [P, *s], F32R) for n, s in WIDTH.items()}
        b1_rows = sb("b1_rows", [P, DH])
        b2_rows, bv_rows, bo_rows, b3_rows = (sb(n, [P, D]) for n in ("b2_rows", "bv_rows", "bo_rows", "b3_rows"))
        bq_col, bk_col = sb("bq_col", [P, DT]), sb("bk_col", [P, DT])
        gamma_col, beta_col = sb("gamma_col", [P, HT]), sb("beta_col", [P, HT])
        shift2_rows = sb("shift2_rows", [P, D])

        def view(tensor, a, b):
            return tensor[:].rearrange("p t c -> p (t c)").rearrange("p (a b) -> p a b", a=a, b=b)

        x1 = sb("x1", [P, NTILE, D])
        adj_f = sb("adj_f", [P, NTILE, N])
        adjT_f = sb("adjT_f", [P, NTILE, N])
        edge_w = sb("edge_w", [P, N])
        h01 = sb("h01", [P, NTILE, D])
        proj = sb("proj", [P, NTILE, 2 * D + 2])
        r = proj[:, :, 0:DH]
        degree = sb("degree", [P, NTILE, 2])
        H = sb("H", [P, NTILE, N], F32R)
        HTr = sb("HTr", [P, NTILE, N], F32R)
        row_count = sb("row_count", [P, NTILE])
        edge_size = sb("edge_size", [P, NTILE])
        node_w = sb("node_w", [P, NTILE])
        diag = sb("diag", [P, NTILE])
        edge_inv, node_inv = sb("edge_inv", [P, NTILE]), sb("node_inv", [P, NTILE])
        inv_tmp = sb("inv_tmp", [P, 2, NTILE])
        gcn_degree = sb("gcn_degree", [P, NTILE])
        fT_hi, fT_lo = sb("fT_hi", [P, DT, N], F32R), sb("fT_lo", [P, DT, N], F32R)
        m_hi, m_lo = sb("m_hi", [P, NTILE, D], F32R), sb("m_lo", [P, NTILE, D], F32R)
        scratch = view(m_lo, DT, N)
        split_hi, split_lo = view(fT_hi, NTILE, D), view(fT_lo, NTILE, D)
        rT_hi = [fT_hi[:, 0], fT_hi[:, 1], view(m_hi, DT, N)[:, 0], view(m_hi, DT, N)[:, 1]]
        rT_lo = [fT_lo[:, 0], fT_lo[:, 1], view(m_lo, DT, N)[:, 0], view(m_lo, DT, N)[:, 1]]

        x2 = sb("x2", [P, NTILE, D])
        adj_b = sb("adj_b", [P, NTILE, N])
        AT = sb("AT", [P, NTILE, N], F32R)
        gcn_scale = sb("gcn_scale", [P, NTILE])
        work = sb("work", [P, NTILE, D])
        bT_hi, bT_lo = sb("bT_hi", [P, DT, N], F32R), sb("bT_lo", [P, DT, N], F32R)
        g_hi, g_lo = sb("g_hi", [P, NTILE, D], F32R), sb("g_lo", [P, NTILE, D], F32R)
        cT_hi, cT_lo = sb("cT_hi", [P, DT, N], F32R), sb("cT_lo", [P, DT, N], F32R)
        ctx_n = sb("ctx_n", [P, NTILE, D])
        qk_hi = [bT_hi, view(g_hi, DT, N)]
        qk_lo = [bT_lo, view(g_lo, DT, N)]
        stacks = [sb("q_stack", [P, 2, DT, N], F32R), sb("k_stack", [P, 2, DT, N], F32R)]
        x3 = sb("x3", [P, NTILE, D])
        v_parts = sb("v_parts", [P, NTILE, HEADS, PARTS, HD], BF16)
        SLOTS = 3
        masked = sb("masked", [P, SLOTS, N])
        top, minus_top = sb("top", [P, NT]), sb("minus_top", [P, NT])
        prob_sum = sb("prob_sum", [P, NT])
        prob_inv = sb("prob_inv", [P, NT])
        probsT_hi, probsT_lo = sb("probsT_hi", [P, 2, N], F16), sb("probsT_lo", [P, 2, N], F16)

        def part_of(tensor, at, a, b):
            flat = tensor[:].rearrange("p t c -> p (t c)")
            return flat[:, at:at + a * b].rearrange("p (a b) -> p a b", a=a, b=b)

        raw = dict(w0=part_of(x3, 0, DT, 2 * D), w1=part_of(work, 0, DT, DH), w2=part_of(ctx_n, 0, HT, D),
                   wq=part_of(adj_b, 0, DT, D), wk=part_of(adj_b, 2 * D, DT, D), wv=part_of(adj_b, 4 * D, DT, D),
                   wo=part_of(adj_b, 6 * D, DT, D), w3=part_of(x2, 0, DT, D))
        mean_w = part_of(masked, HT * D, 1, P)[:, 0]
        w2g = part_of(masked, 0, HT, D)

        loaded = sem("loaded")
        ident_zero, ident_done, consts = sem("ident_zero"), sem("ident_done"), sem("consts")
        gamma_done, mean_done, shift_done, centred = (
            sem(n) for n in ("gamma_done", "mean_done", "shift_done", "centred"))
        wq_scaled, uppers = sem("wq_scaled"), sem("uppers")
        passed = sem("passed")
        ready = sem("ready")
        READY = len(WIDTH) + 2

        x_loaded, adjT_loaded, adj_loaded, edge_w_loaded, adj_b_loaded = (
            signal(n, DMA) for n in ("x_loaded", "adjT_loaded", "adj_loaded", "edge_w_loaded", "adj_b_loaded"))
        stored = signal("stored", DMA)
        PAIR_DMAS = 8
        stacked = [signal(f"stacked{i}", 2 * PAIR_DMAS * DMA) for i in range(2)]

        class Norm:

            def __init__(self, name):
                self.stats = sb(f"{name}_stats", [P, NTILE, 6])
                self.mv = sb(f"{name}_mv", [P, NTILE, 2])
                self.var = sb(f"{name}_var", [P, NTILE])
                self.neg = sb(f"{name}_neg", [P, NTILE])
                self.rstd = sb(f"{name}_rstd", [P, NTILE])
                self.shift = sb(f"{name}_shift", [P, NTILE])
                self.stats_done = signal(f"{name}_stats_done", NTILE)
                self.mv_done = signal(f"{name}_mv_done", NTILE)
                self.prep_done = signal(f"{name}_prep_done", 2)
                self.rstd_done = signal(f"{name}_rstd_done")
                self.shift_done = signal(f"{name}_shift_done")
                self.done = signal(f"{name}_done", NTILE)

        norm0, norm1, norm_r, norm2, norm3 = (Norm(n) for n in ("norm0", "norm1", "norm_r", "norm2", "norm3"))
        UPPER_TURN0, UPPER_EDGES1, UPPER_NODES1, UPPER_TURN1, UPPER_EDGES2 = 0, 2, 6, 8, 12
        front_upper = signal("front_upper", 16)
        UPPER_TURN2, UPPER_QUERIES = 0, 2
        back_upper = signal("back_upper", 6)
        UPPER_TURN_CTX, UPPER_TURN3, UPPER_PROJECT3 = 0, 2, 4
        late_upper = signal("late_upper", 8)
        degree_floor, degree_inv = signal("degree_floor", NTILE), signal("degree_inv", NTILE)
        x1_done = signal("x1_done")
        masks_done = signal("masks_done", 4 * NTILE)
        inv_floor, inv_recip, inv_done = signal("inv_floor", 2), signal("inv_recip"), signal("inv_done", 2)
        gcn_degree_done = signal("gcn_degree_done")
        h1_upper, h1_lower = signal("h1_upper", NTILE), signal("h1_lower")
        base1_half, base1_done = signal("base1_half"), signal("base1_done")
        relu_done = signal("relu_done", NTILE)
        p_upper, p_lower = signal("p_upper"), signal("p_lower")
        AT_copied, AT_done, gcn_scale_done = signal("AT_copied"), signal("AT_done", NTILE), signal("gcn_scale_done")
        v_part1, v_rest1, v_part2, v_part3 = (signal(n) for n in ("v_part1", "v_rest1", "v_part2", "v_part3"))
        neg_done, exp_done = signal("neg_done", NT), signal("exp_done", NT)
        probsT_upper = signal("probsT_upper", NT)
        context_done = signal("context_done", NT)
        prob_inv_done, ctx_done = signal("prob_inv_done", HEADS), signal("ctx_done", HEADS)
        base2_done = signal("base2_done")
        tanh_done, result_done = signal("tanh_done", 2), signal("result_done", 2)

        block = ctx.enter_context(nc.Block())

        WEIGHTS = [
            (raw["w1"], w1T.rearrange("(kt p) h -> p kt h", p=P)),
            (raw["w2"], w2T.rearrange("(kt p) o -> p kt o", p=P)),
            (raw["wq"], wqT.rearrange("(kt p) o -> p kt o", p=P)),
            (raw["wk"], wkT.rearrange("(kt p) o -> p kt o", p=P)),
            (raw["wv"], wvT.rearrange("(kt p) o -> p kt o", p=P)),
            (raw["wo"], woT.rearrange("(kt p) o -> p kt o", p=P)),
            (raw["w3"], w3.rearrange("(kt p) o -> p kt o", p=P)),
            (b1_rows, b1.partition_broadcast(P)),
            (b2_rows, b2.partition_broadcast(P)),
            (bv_rows, bv.partition_broadcast(P)),
            (bo_rows, bo.partition_broadcast(P)),
            (b3_rows, b3.partition_broadcast(P)),
            (bq_col, bq_cols),
            (bk_col, bk_cols),
            (gamma_col, gamma_cols),
            (beta_col, beta_cols),
        ]
        w0_v = w0T.rearrange("(half kt p) o -> p half kt o", half=2, p=P)
        LOADS = len(WEIGHTS) + 2
        x_v = x.rearrange("b (t p) f -> b p t f", p=P)
        out_v = out.rearrange("b (t p) f -> b p t f", p=P)
        adj_v = adj.rearrange("b (t p) j -> b p t j", p=P)
        adjT_v = adjT.rearrange("b (t p) j -> b p t j", p=P)

        def f32(ap):
            return ap.bitcast(F32)

        def wait_alone(eng, signal, b, n):
            wait(eng, signal, b, n)
            eng.sem_inc(passed, 1)

        def program(eng, engine, steps):

            def run(i, groups):
                for group, name, n in body(engine, groups):
                    if name in steps:
                        steps[name](i + GROUPS[group], n)

            run(-1, ["front"])
            run(0, ["back", "front"])
            with eng.Fori(1, B - 1) as i:
                run(i, ["late", "back", "front"])
            run(B - 1, ["late", "back"])
            run(B, ["late"])

        def cols(t):
            return slice(t * P, (t + 1) * P)

        def pair(g):
            return slice(2 * g, 2 * g + 2)

        def halves(tile):
            return tile[:].rearrange("p (t c) -> p t c", c=D)

        def rows4(rows, n):
            return rows[:].rearrange("p (o d) -> p o d", o=1).broadcast_to([P, n, D])

        def head_of(t):
            return (t // 4) % 2 * PER_TILE + t // 8

        @block.sync
        def _(sp):
            for half in range(2):
                sp.dma_start(raw["w0"][:, :, half * D:(half + 1) * D], w0_v[:, half]).then_inc(loaded, DMA)
            for dst, src in WEIGHTS:
                sp.dma_start(dst[:] if not isinstance(dst, bass.AP) else dst, src).then_inc(loaded, DMA)

            def load_front(b):
                for k in range(2):
                    wait_for_earlier_batches(sp, front.drained[k], b)
                sp.dma_start(x1[:], x_v[b]).then_inc(x_loaded.semaphore, DMA)
                wait_for_earlier_batches(sp, masks_done, b)
                sp.dma_start(adjT_f[:], adjT_v[b]).then_inc(adjT_loaded.semaphore, DMA)
                sp.dma_start(adj_f[:], adj_v[b]).then_inc(adj_loaded.semaphore, DMA)
                sp.dma_start(edge_w[:], adj[b, 0].partition_broadcast(P)).then_inc(edge_w_loaded.semaphore, DMA)

            def load_back(b):
                if not (isinstance(b, int) and b == 0):
                    for t in (NT - 2, NT - 1):
                        back.wait_drained(sp, b - 1, B_SCORES + t)
                sp.dma_start(adj_b[:], adj_v[b]).then_inc(adj_b_loaded.semaphore, DMA)

            def stack(b, j):
                if j >= 2:
                    for t in (8 * (j - 1) - 2, 8 * (j - 1) - 1):
                        back.wait_drained(sp, b, B_SCORES + t)
                for which, groups, first in ((0, "hhll", B_QUERIES), (1, "hlhl", B_KEYS)):
                    if j == 0:
                        for t in range(DT):
                            back.wait_drained(sp, b, first + t)
                    for g, part in enumerate(groups):
                        src = (qk_hi if part == "h" else qk_lo)[which]
                        sp.dma_start(stacks[which][HD * g:HD * (g + 1), j % 2].bitcast(F32),
                                     src[HD * j:HD * (j + 1)].bitcast(F32)).then_inc(
                                         stacked[j % 2].semaphore, DMA)

            def store(b):
                wait(sp, result_done, b, 2)
                sp.dma_start(out_v[b], x3[:]).then_inc(stored.semaphore, DMA)

            def back_half(b):
                load_back(b)
                for j in range(PER_TILE):
                    stack(b, j)
                    if j == 0 and not (isinstance(b, int) and b == 0):
                        store(b - 1)

            load_front(0)
            sp.wait_ge(ready, READY)
            load_front(1)
            back_half(0)
            with sp.Fori(1, B - 1) as i:
                load_front(i + 1)
                back_half(i)
            back_half(B - 1)
            store(B - 1)
            wait(sp, stored, B - 1, DMA)

        @block.tensor
        def _(pe):
            def transpose_tiles(bank, b, u, source, t, count):
                tile = bank.tile(u)
                for s in range(count):
                    last = nc.tensor.transpose(tile[:, s * P:(s + 1) * P], source[:, s, t * P:(t + 1) * P], ident[:])
                bank.fill(last, u)

            def split_product(dst, terms):
                n = len(terms)
                for i, (lh, ll, rh, rl) in enumerate(terms):
                    nc.tensor.matmul(dst, lh, rh, start=(i == 0), stop=False)
                    nc.tensor.matmul(dst, lh, rl, start=False, stop=False)
                    last = nc.tensor.matmul(dst, ll, rh, start=False, stop=(i == n - 1))
                return last

            def mask_product(dst, terms):
                n = len(terms)
                for i, (a, hi, lo, mask_left) in enumerate(terms):
                    for k, part in enumerate((hi, lo)):
                        l, rr = (a, part) if mask_left else (part, a)
                        last = nc.tensor.matmul(dst, l, rr, start=(i == 0 and k == 0), stop=(i == n - 1 and k == 1))
                return last

            pe.wait_ge(ident_done, 1)
            pe.wait_ge(consts, CONSTS)
            pe.wait_ge(loaded, LOADS * DMA)
            pe.wait_ge(gamma_done, HT)
            for kt in range(HT):
                last = nc.tensor.matmul(front.tiles[0][:, 0:D], mean_w, w2g[:, kt, :],
                                        start=(kt == 0), stop=(kt == HT - 1))
            last.then_inc(mean_done, 1)
            for kt in range(HT):
                last = nc.tensor.matmul(front.tiles[1][:, 0:D], beta_col[:, kt:kt + 1].broadcast_to([P, P]),
                                        raw["w2"][:, kt, :], start=(kt == 0), stop=(kt == HT - 1))
            last.then_inc(shift_done, 1)
            pe.wait_ge(ready, READY)

            def turn0(b, t):
                wait(pe, norm0.done, b, NTILE)
                front.wait_free(pe, b, F_TURN0 + t)
                transpose_tiles(front, b, F_TURN0 + t, h01, t, NTILE)

            def project0(b, s):
                u = F_PROJECT0 + s
                front.wait_read_out(pe, b, [F_TURN0, F_TURN0 + 1] if s == 0 else [], u)
                last = split_product(front.tile(u)[:], [
                    (fT_hi[:, k, cols(s)], fT_lo[:, k, cols(s)], w_hi["w0"][:, k, :], w_lo["w0"][:, k, :])
                    for k in range(DT)])
                front.fill(last, u)

            def aggregate0(b, t):
                u = F_AGG0 + t
                if t == 0:
                    wait(pe, adjT_loaded, b, DMA)
                front.wait_read_out(pe, b, [F_PROJECT0 + s for s in range(NTILE)] if t == 0 else [], u)
                for k in range(NTILE):
                    last = nc.tensor.matmul(front.tile(u)[:, 0:D + 1], adjT_f[:, k, cols(t)],
                                            proj[:, k, D:2 * D + 1], start=(k == 0), stop=(k == NTILE - 1))
                front.fill(last, u)

            def gather(bank, b, u, matrix, hi, lo, g):
                for half in range(2):
                    last = mask_product(bank.tile(u)[:, half * D:(half + 1) * D], [
                        (matrix[:, k, cols(2 * g + half)], hi[:, k, :], lo[:, k, :], True) for k in range(NTILE)])
                bank.fill(last, u)

            def edges1(b, g):
                wait(pe, masks_done, b, 4 * NTILE)
                wait(pe, h1_upper, b, NTILE)
                wait(pe, h1_lower, b, 1)
                front.wait_free(pe, b, F_EDGES1 + g)
                gather(front, b, F_EDGES1 + g, H, split_hi, split_lo, g)

            def nodes1(b, t):
                u = F_NODES1 + t
                front.wait_read_out(pe, b, [F_EDGES1, F_EDGES1 + 1] if t == 0 else [], u)
                last = mask_product(front.tile(u)[:], [
                    (HTr[:, k, :], m_hi[:, k, cols(t)], m_lo[:, k, cols(t)], False) for k in range(NTILE)])
                front.fill(last, u)

            def expand1(b, s):
                u = F_EXPAND1 + s
                front.wait_read_out(pe, b, [F_NODES1, F_NODES1 + 1] if s == 0 else [], u)
                last = split_product(front.tile(u)[:], [
                    (fT_hi[:, k, cols(s)], fT_lo[:, k, cols(s)], w_hi["w1"][:, k, :], w_lo["w1"][:, k, :])
                    for k in range(DT)])
                front.fill(last, u)

            def turn1(b, t):
                wait(pe, relu_done, b, NTILE)
                front.wait_free(pe, b, F_TURN1 + t)
                transpose_tiles(front, b, F_TURN1 + t, r, t, NTILE)

            def contract1(b, g):
                u = F_CONTRACT1 + g
                front.wait_read_out(pe, b, [F_TURN1 + t for t in range(HT)] if g == 0 else [], u)
                for half in range(2):
                    s = 2 * g + half
                    last = split_product(front.tile(u)[:, half * D:(half + 1) * D], [
                        (rT_hi[k][:, cols(s)], rT_lo[k][:, cols(s)], w_hi["w2"][:, k, :], w_lo["w2"][:, k, :])
                        for k in range(HT)])
                front.fill(last, u)

            def edges2(b, g):
                wait(pe, p_upper, b, 1)
                wait(pe, p_lower, b, 1)
                front.wait_free(pe, b, F_EDGES2 + g)
                gather(front, b, F_EDGES2 + g, H, split_hi, split_lo, g)

            def nodes2(b, g):
                front.wait_read_out(pe, b, [F_EDGES2, F_EDGES2 + 1] if g == 0 else [], F_NODES2 + g)
                gather(front, b, F_NODES2 + g, HTr, m_hi, m_lo, g)

            def turn2(b, t):
                wait(pe, norm2.done, b, NTILE)
                back.wait_free(pe, b, B_TURN2 + t)
                transpose_tiles(back, b, B_TURN2 + t, ctx_n, t, NTILE)

            def project_qk(b, u, name, t):
                back.wait_read_out(pe, b, [B_TURN2, B_TURN2 + 1], u)
                last = split_product(back.tile(u)[:], [
                    (w_hi[name][:, k, cols(t)], w_lo[name][:, k, cols(t)], cT_hi[:, k, :], cT_lo[:, k, :])
                    for k in range(DT)])
                back.fill(last, u)

            def project_rows(bank, b, u, hi, lo, name, g):
                for half in range(2):
                    s = 2 * g + half
                    last = split_product(bank.tile(u)[:, half * D:(half + 1) * D], [
                        (hi[:, k, cols(s)], lo[:, k, cols(s)], w_hi[name][:, k, :], w_lo[name][:, k, :])
                        for k in range(DT)])
                bank.fill(last, u)

            def values(b, g):
                back.wait_free(pe, b, B_VALUES + g)
                project_rows(back, b, B_VALUES + g, cT_hi, cT_lo, "wv", g)

            def scores(b, t):
                j, mt, qt = t // 8, t // 4 % 2, t % 4
                if t % 8 == 0:
                    wait(pe, stacked[j % 2], b, (j // 2 + 1) * PAIR_DMAS * DMA)
                u = B_SCORES + t
                back.wait_free(pe, b, u)
                back.fill(nc.tensor.matmul(back.tile(u)[:], stacks[0][:, j % 2, mt, cols(qt)],
                                           stacks[1][:, j % 2, mt, :], start=True, stop=True), u)

            def probs_turn(b, t):
                wait(pe, exp_done, b, t + 1)
                turned.wait_free(pe, b, t)
                for k in range(NTILE):
                    last = nc.tensor.transpose(turned.tile(t)[:, cols(k)], masked[:, t % SLOTS, cols(k)], ident[:])
                turned.fill(last, t)

            def context(b, t):
                if t == 0:
                    wait(pe, v_part1, b, 1)
                    wait(pe, v_part2, b, 1)
                    wait(pe, v_part3, b, 1)
                if t % 4 == 0:
                    mixed.wait_free(pe, b, t // 4)
                turned.wait_drained(pe, b, t)
                dst = mixed.tile(t // 4)[:, (t % 4) * PARTS * HD:(t % 4 + 1) * PARTS * HD]
                for k in range(NTILE):
                    for part in (probsT_hi, probsT_lo):
                        last = nc.tensor.matmul(dst, part[:, t % 2, cols(k)], v_parts[:, k, head_of(t)].rearrange("p c d -> p (c d)"),
                                                start=(k == 0 and part is probsT_hi),
                                                stop=(k == NTILE - 1 and part is probsT_lo))
                last.then_inc(context_done.semaphore, 1)

            def turn_ctx(b, t):
                wait(pe, ctx_done, b, HEADS)
                turned.wait_free(pe, b, T_TURN_CTX + t)
                transpose_tiles(turned, b, T_TURN_CTX + t, ctx_n, t, NTILE)

            def output2(b, g):
                turned.wait_read_out(pe, b, [T_TURN_CTX, T_TURN_CTX + 1] if g == 0 else [], T_OUTPUT2 + g)
                project_rows(turned, b, T_OUTPUT2 + g, cT_hi, cT_lo, "wo", g)

            def turn3(b, t):
                wait(pe, norm3.done, b, NTILE)
                turned.wait_free(pe, b, T_TURN3 + t)
                transpose_tiles(turned, b, T_TURN3 + t, work, t, NTILE)

            def project3(b, g):
                turned.wait_read_out(pe, b, [T_TURN3, T_TURN3 + 1] if g == 0 else [], T_PROJECT3 + g)
                project_rows(turned, b, T_PROJECT3 + g, bT_hi, bT_lo, "w3", g)

            def aggregate3(b, g):
                wait(pe, AT_done, b, NTILE)
                turned.wait_read_out(pe, b, [T_PROJECT3, T_PROJECT3 + 1] if g == 0 else [], T_AGG3 + g)
                gather(turned, b, T_AGG3 + g, AT, g_hi, g_lo, g)

            program(pe, "tensor", {
                "turn0": turn0, "project0": project0, "aggregate0": aggregate0,
                "edges1": edges1, "nodes1": nodes1, "expand1": expand1, "turn1": turn1,
                "contract1": contract1, "edges2": edges2, "nodes2": nodes2,
                "turn2": turn2,
                "queries": lambda b, t: project_qk(b, B_QUERIES + t, "wq", t),
                "keys": lambda b, t: project_qk(b, B_KEYS + t, "wk", t),
                "values": values,
                "scores": scores, "probs": probs_turn, "context": context,
                "turn_ctx": turn_ctx, "output2": output2,
                "turn3": turn3, "project3": project3, "aggregate3": aggregate3,
            })

        @block.vector
        def _(ve):
            nv = nc.vector

            ve.wait_ge(loaded, LOADS * DMA)
            for k in range(HT):
                nv.tensor_scalar(w2g[:, k], raw["w2"][:, k], gamma_col[:, k:k + 1], None, ALU.mult).then_inc(gamma_done, 1)
            others = [n for n in WIDTH if n != "w2"]
            nv.tensor_scalar(raw["wq"], raw["wq"], SCORE_SCALE, None, ALU.mult).then_inc(wq_scaled, 1)
            ve.wait_ge(wq_scaled, 1)
            for n in others:
                nv.tensor_copy(w_hi[n][:], raw[n]).then_inc(uppers, 1)
            nv.tensor_scalar(bq_col[:], bq_col[:], SCORE_SCALE, None, ALU.mult).then_inc(ready, 1)
            ve.wait_ge(uppers, len(others))
            for n in others:
                nv.tensor_tensor(w_lo[n][:], raw[n], f32(w_hi[n][:]), ALU.subtract).then_inc(ready, 1)
            ve.wait_ge(gamma_done, HT)
            ve.wait_ge(mean_done, 1)
            for k in range(HT):
                nv.tensor_tensor(w2g[:, k], w2g[:, k], front.tiles[0][:, 0:D], ALU.subtract).then_inc(centred, 1)
            ve.wait_ge(centred, HT)
            nv.tensor_copy(w_hi["w2"][:], w2g).then_inc(uppers, 1)
            ve.wait_ge(uppers, len(others) + 1)
            nv.tensor_tensor(w_lo["w2"][:], w2g, f32(w_hi["w2"][:]), ALU.subtract).then_inc(ready, 1)
            ve.wait_ge(shift_done, 1)
            nv.tensor_copy(shift2_rows[:], front.tiles[1][:, 0:D]).then_inc(ready, 1)
            ve.wait_ge(consts, CONSTS)
            ve.wait_ge(ident_done, 1)

            def statistics(norm, b, source):
                for t in range(NTILE):
                    nv.bn_stats(norm.stats[:, t], source[:, t]).then_inc(norm.stats_done.semaphore, 1)
                wait_alone(ve, norm.stats_done, b, NTILE)
                for t in range(NTILE):
                    nv.bn_aggr(norm.mv[:, t], norm.stats[:, t]).then_inc(norm.mv_done.semaphore, 1)

            def lower(bank, b, u, upper, n, dst, hi, source=None, scale=None):
                wait(ve, upper, b, n)
                source = bank.tile(u)[:] if source is None else source
                if scale is None:
                    return nv.tensor_tensor(dst, source, f32(hi), ALU.subtract)
                return nv.scalar_tensor_tensor(dst, source, scale, f32(hi), ALU.mult, ALU.subtract)

            def norm0_(b, _):
                wait(ve, x_loaded, b, DMA)
                statistics(norm0, b, x1)

            def turn0(b, t):
                u = F_TURN0 + t
                front.drain(lower(front, b, u, front_upper, UPPER_TURN0 + t + 1, fT_lo[:, t], fT_hi[:, t]), u)

            def aggregate0(b, t):
                u = F_AGG0 + t
                tile = front.tile(u)
                front.wait_filled(ve, b, u)
                nv.tensor_scalar(degree[:, t, 0:1], tile[:, D:D + 1], DEG_EPS, None, ALU.max).then_inc(
                    degree_floor.semaphore, 1)
                wait(ve, degree_floor, b, t + 1)
                nv.reciprocal(degree[:, t, 1:2], degree[:, t, 0:1]).then_inc(degree_inv.semaphore, 1)
                wait(ve, degree_inv, b, t + 1)
                front.drain(nv.scalar_tensor_tensor(h01[:, t], tile[:, 0:D], degree[:, t, 1:2], proj[:, t, 0:D],
                                                    ALU.mult, ALU.add), u)
                if t == NTILE - 1:
                    for k in (NTILE - 2, NTILE - 1):
                        front.wait_drained(ve, b, F_AGG0 + k)
                    nv.scalar_tensor_tensor(x1[:], h01[:], 0.0, x1[:], ALU.max, ALU.add).then_inc(
                        x1_done.semaphore, 1)

            def masks(b, t):
                if t == 0:
                    wait(ve, adj_loaded, b, DMA)
                    wait(ve, adjT_loaded, b, DMA)
                    wait(ve, edge_w_loaded, b, DMA)
                nv.tensor_scalar(H[:, t], adj_f[:, t], 0.0, 0.0, ALU.not_equal, ALU.add,
                                 accum_out=row_count[:, t:t + 1]).then_inc(masks_done.semaphore, 1)
                nv.tensor_scalar(HTr[:, t], adjT_f[:, t], 0.0, 0.0, ALU.not_equal, ALU.add,
                                 accum_out=edge_size[:, t:t + 1]).then_inc(masks_done.semaphore, 1)
                if t > 0:
                    wait(ve, masks_done, b, 4 * t)
                nv.scalar_tensor_tensor(scratch[:, 0], adj_f[:, t], 0.0, edge_w[:], ALU.not_equal, ALU.mult,
                                        accum_out=node_w[:, t:t + 1]).then_inc(masks_done.semaphore, 1)
                nv.scalar_tensor_tensor(scratch[:, 1, 0:P], adj_f[:, t, cols(t)], 0.0, ident[:], ALU.not_equal,
                                        ALU.mult, accum_out=diag[:, t:t + 1]).then_inc(masks_done.semaphore, 1)
                if t == NTILE - 1:
                    inverses(b)

            def inverses(b):
                wait(ve, masks_done, b, 4 * NTILE - 1)
                nv.tensor_scalar(inv_tmp[:, 0], edge_size[:], 1.0, None, ALU.max).then_inc(inv_floor.semaphore, 1)
                nv.tensor_scalar(inv_tmp[:, 1], node_w[:], TINY, None, ALU.max).then_inc(inv_floor.semaphore, 1)
                wait(ve, inv_floor, b, 2)
                nv.reciprocal(inv_tmp[:], inv_tmp[:]).then_inc(inv_recip.semaphore, 1)
                wait(ve, inv_recip, b, 1)
                nv.scalar_tensor_tensor(edge_inv[:], edge_size[:], 0.0, inv_tmp[:, 0], ALU.is_gt, ALU.mult).then_inc(
                    inv_done.semaphore, 1)
                nv.scalar_tensor_tensor(node_inv[:], node_w[:], 0.0, inv_tmp[:, 1], ALU.is_gt, ALU.mult).then_inc(
                    inv_done.semaphore, 1)
                wait(ve, masks_done, b, 4 * NTILE)
                wait_for_earlier_batches(ve, gcn_scale_done, b)
                nv.scalar_tensor_tensor(gcn_degree[:], row_count[:], 1.0, diag[:], ALU.add, ALU.subtract).then_inc(
                    gcn_degree_done.semaphore, 1)

            def norm1_(b, _):
                wait(ve, x1_done, b, 1)
                statistics(norm1, b, x1)

            def edges(b, g, first_use, first_upper):
                u = first_use + g
                for half in range(2):
                    e = 2 * g + half
                    last = lower(front, b, u, front_upper, first_upper + 2 * g + 2, m_lo[:, e], m_hi[:, e],
                                 halves(front.tile(u))[:, half], edge_inv[:, e:e + 1])
                front.drain(last, u)

            def nodes1(b, t):
                u = F_NODES1 + t
                front.drain(lower(front, b, u, front_upper, UPPER_NODES1 + t + 1, fT_lo[:, t], fT_hi[:, t]), u)

            def expand1(b, s):
                u = F_EXPAND1 + s
                front.wait_filled(ve, b, u)
                front.drain(nv.scalar_tensor_tensor(r[:, s], front.tile(u)[:], node_inv[:, s:s + 1], b1_rows[:],
                                                    ALU.mult, ALU.add), u)

            def norm_r_(b, _):
                wait(ve, relu_done, b, NTILE)
                statistics(norm_r, b, r)

            def turn1(b, t):
                u = F_TURN1 + t
                front.drain(lower(front, b, u, front_upper, UPPER_TURN1 + t + 1, rT_lo[t], rT_hi[t]), u)

            def contract1(b, g):
                u = F_CONTRACT1 + g
                wait(ve, norm_r.rstd_done, b, 1)
                wait(ve, base1_done, b, 1)
                front.wait_filled(ve, b, u)
                for half in range(2):
                    s = 2 * g + half
                    last = nv.scalar_tensor_tensor(h01[:, s], halves(front.tile(u))[:, half],
                                                   norm_r.rstd[:, s:s + 1], shift2_rows[:], ALU.mult, ALU.add)
                front.drain(last, u)

            def nodes2(b, g):
                u = F_NODES2 + g
                if g == 0 and not (isinstance(b, int) and b == 0):
                    for k in range(2):
                        turned.wait_drained(ve, b - 1, T_OUTPUT2 + k)
                front.wait_filled(ve, b, u)
                for half in range(2):
                    s = 2 * g + half
                    last = nv.scalar_tensor_tensor(x2[:, s], halves(front.tile(u))[:, half], node_inv[:, s:s + 1],
                                                   x1[:, s], ALU.mult, ALU.add)
                front.drain(last, u)

            def norm2_(b, _):
                for g in range(2):
                    front.wait_drained(ve, b, F_NODES2 + g)
                statistics(norm2, b, x2)

            def keep(b, _):
                wait(ve, AT_copied, b, 1)
                for t in range(NTILE):
                    nv.tensor_tensor(AT[:, t, cols(t)], f32(AT[:, t, cols(t)]), ident[:], ALU.max).then_inc(
                        AT_done.semaphore, 1)

            def turn_lower(bank, upper, b, t, first_use, first_upper, dst_lo, dst_hi, scale=None):
                u = first_use + t
                bank.drain(lower(bank, b, u, upper, first_upper + t + 1, dst_lo[:, t], dst_hi[:, t],
                                 scale=scale), u)

            def qk_lower(b, u, which, t, bias):
                wait(ve, back_upper, b, UPPER_QUERIES + u - B_QUERIES + 1)
                back.drain(nv.scalar_tensor_tensor(qk_lo[which][:, t], back.tile(u)[:], bias[:, t:t + 1],
                                                   f32(qk_hi[which][:, t]), ALU.add, ALU.subtract), u)

            def values(b, g):
                u = B_VALUES + g
                back.wait_filled(ve, b, u)
                back.drain(nv.tensor_tensor(ctx_n[:, pair(g)], halves(back.tile(u)), rows4(bv_rows, 2), ALU.add), u)

            def value_parts(b, _):
                for g in range(2):
                    back.wait_drained(ve, b, B_VALUES + g)
                wait_for_earlier_batches(ve, context_done, b)
                nv.tensor_copy(v_parts[:, :, :, 0], ctx_n[:].rearrange("p t (h d) -> p t h d", d=HD)).then_inc(
                    v_part1.semaphore, 1)
                wait(ve, v_rest1, b, 1)
                nv.tensor_copy(v_parts[:, :, :, 1], ctx_n[:].rearrange("p t (h d) -> p t h d", d=HD)).then_inc(
                    v_part2.semaphore, 1)

            def scores(b, t):
                u = B_SCORES + t
                if t == 0:
                    wait(ve, adj_b_loaded, b, DMA)
                if t >= SLOTS:
                    turned.wait_filled(ve, b, t - SLOTS)
                back.wait_filled(ve, b, u)
                ve.sem_inc(passed, 1)
                back.drain(nv.tensor_tensor_reduce(out=masked[:, t % SLOTS], in0=back.tile(u)[:],
                                                   in1=adj_b[:, t % 4], scale=1.0, scalar=-3e38, op0=ALU.mult,
                                                   op1=ALU.max, accum_out=top[:, t:t + 1]), u)

            def probs(b, t):
                wait(ve, probsT_upper, b, t + 1)
                turned.drain(nv.scalar_tensor_tensor(probsT_lo[:, t % 2], turned.tile(t)[:], PROB_SCALE,
                                                     probsT_hi[:, t % 2], ALU.mult, ALU.subtract), t)

            def weigh(b, h):
                wait(ve, context_done, b, 4 * (h + 1))
                head = head_of(4 * h)
                dst = ctx_n[:, :, head * HD:(head + 1) * HD]
                src = mixed.tile(h)[:, 0:NTILE * PARTS * HD].rearrange("p (q c d) -> p q d c", q=NTILE, c=PARTS)
                mixed.drain(nv.tensor_reduce(dst, src, AX_X, ALU.add), h)
                wait(ve, exp_done, b, 4 * (h + 1))
                nv.reciprocal(prob_inv[:, 4 * h:4 * h + 4], prob_sum[:, 4 * h:4 * h + 4]).then_inc(
                    prob_inv_done.semaphore, 1)
                mixed.wait_drained(ve, b, h)
                wait(ve, prob_inv_done, b, h + 1)
                inv = prob_inv[:, 4 * h:4 * h + 4].rearrange("p (q o) -> p q o", o=1).broadcast_to([P, NTILE, HD])
                nv.tensor_tensor(dst, dst, inv, ALU.mult).then_inc(ctx_done.semaphore, 1)

            def output2(b, g):
                u = T_OUTPUT2 + g
                wait(ve, base2_done, b, 1)
                wait_for_earlier_batches(ve, stored, b)
                turned.wait_filled(ve, b, u)
                turned.drain(nv.tensor_tensor(x3[:, pair(g)], halves(turned.tile(u)), x2[:, pair(g)], ALU.add), u)

            def norm3_(b, _):
                for g in range(2):
                    turned.wait_drained(ve, b, T_OUTPUT2 + g)
                statistics(norm3, b, x3)

            def project3(b, g):
                u = T_PROJECT3 + g
                for half in range(2):
                    s = 2 * g + half
                    last = lower(turned, b, u, late_upper, UPPER_PROJECT3 + 2 * g + 2, g_lo[:, s], g_hi[:, s],
                                 halves(turned.tile(u))[:, half], gcn_scale[:, s:s + 1])
                turned.drain(last, u)

            def aggregate3(b, g):
                u = T_AGG3 + g
                turned.wait_filled(ve, b, u)
                for half in range(2):
                    s = 2 * g + half
                    last = nv.scalar_tensor_tensor(work[:, s], halves(turned.tile(u))[:, half],
                                                   gcn_scale[:, s:s + 1], b3_rows[:], ALU.mult, ALU.add)
                turned.drain(last, u)

            program(ve, "vector", {
                "norm0": norm0_, "turn0": turn0, "aggregate0": aggregate0, "masks": masks, "norm1": norm1_,
                "edges1": lambda b, g: edges(b, g, F_EDGES1, UPPER_EDGES1), "nodes1": nodes1,
                "expand1": expand1, "norm_r": norm_r_, "turn1": turn1, "contract1": contract1,
                "edges2": lambda b, g: edges(b, g, F_EDGES2, UPPER_EDGES2), "nodes2": nodes2,
                "norm2": norm2_, "keep": keep,
                "turn2": lambda b, t: turn_lower(back, back_upper, b, t, B_TURN2, UPPER_TURN2, cT_lo, cT_hi),
                "queries": lambda b, t: qk_lower(b, B_QUERIES + t, 0, t, bq_col),
                "keys": lambda b, t: qk_lower(b, B_KEYS + t, 1, t, bk_col),
                "values": values, "value_parts": value_parts, "scores": scores, "probs": probs, "weigh": weigh,
                "turn_ctx": lambda b, t: turn_lower(turned, late_upper, b, t, T_TURN_CTX, UPPER_TURN_CTX,
                                                    cT_lo, cT_hi, 1.0 / PROB_SCALE),
                "output2": output2, "norm3": norm3_,
                "turn3": lambda b, t: turn_lower(turned, late_upper, b, t, T_TURN3, UPPER_TURN3, bT_lo, bT_hi),
                "project3": project3, "aggregate3": aggregate3,
            })

        @block.scalar
        def _(ac):
            act = nc.scalar.activation
            ac.wait_ge(ready, READY)
            ac.wait_ge(consts, CONSTS)

            def normalise(norm, b, dst, source):
                wait(ac, norm.rstd_done, b, 1)
                wait(ac, norm.shift_done, b, 1)
                for t in range(NTILE):
                    act(dst[:, t], source[:, t], ACT.Relu, bias=norm.shift[:, t:t + 1],
                        scale=norm.rstd[:, t:t + 1]).then_inc(norm.done.semaphore, 1)

            def upper(bank, b, u, dst, signal, source=None, scale=1.0):
                bank.wait_filled(ac, b, u)
                act(dst, bank.tile(u)[:] if source is None else source, ACT.Copy,
                    scale=scale).then_inc(signal.semaphore, 1)

            def project0(b, s):
                u = F_PROJECT0 + s
                front.wait_filled(ac, b, u)
                front.drain(act(proj[:, s, 0:2 * D], front.tile(u)[:], ACT.Copy), u)

            def edges(b, g, first_use):
                wait(ac, inv_done, b, 2)
                u = first_use + g
                for half in range(2):
                    e = 2 * g + half
                    upper(front, b, u, m_hi[:, e], front_upper, halves(front.tile(u))[:, half],
                          edge_inv[:, e:e + 1])

            def expand1(b, s):
                front.wait_drained(ac, b, F_EXPAND1 + s)
                act(r[:, s], r[:, s], ACT.Relu).then_inc(relu_done.semaphore, 1)

            def split2(b, _):
                for g in range(2):
                    front.wait_filled(ac, b, F_CONTRACT1 + g)
                    front.wait_drained(ac, b, F_CONTRACT1 + g)
                act(split_hi, h01[:], ACT.Copy).then_inc(p_upper.semaphore, 1)

            def keep(b, _):
                wait(ac, masks_done, b, 4 * NTILE)
                act(AT[:], f32(HTr[:]), ACT.Copy).then_inc(AT_copied.semaphore, 1)

            def split1(b, _):
                for t in range(NTILE):
                    wait(ac, norm1.done, b, t + 1)
                    act(split_hi[:, t], h01[:, t], ACT.Copy).then_inc(h1_upper.semaphore, 1)

            def norm2_(b, _):
                normalise(norm2, b, ctx_n, x2)

            def qk(b, u, which, t, bias):
                back.wait_filled(ac, b, u)
                act(qk_hi[which][:, t], back.tile(u)[:], ACT.Identity,
                    bias=bias[:, t:t + 1]).then_inc(back_upper.semaphore, 1)

            def scores(b, t):
                back.wait_drained(ac, b, B_SCORES + t)
                act(minus_top[:, t:t + 1], top[:, t:t + 1], ACT.Copy, scale=-1.0).then_inc(neg_done.semaphore, 1)
                wait(ac, neg_done, b, t + 1)
                act(masked[:, t % SLOTS], masked[:, t % SLOTS], ACT.Exp, bias=minus_top[:, t:t + 1],
                    accum_out=prob_sum[:, t:t + 1]).then_inc(exp_done.semaphore, 1)

            def probs(b, t):
                if not (isinstance(b, int) and b == 0 and t < 2):
                    wait(ac, context_done, b, max(t - 1, 0))
                turned.wait_filled(ac, b, t)
                act(probsT_hi[:, t % 2], turned.tile(t)[:], ACT.Copy, scale=PROB_SCALE).then_inc(
                    probsT_upper.semaphore, 1)

            def project3(b, g):
                wait(ac, gcn_scale_done, b, 1)
                u = T_PROJECT3 + g
                for half in range(2):
                    s = 2 * g + half
                    upper(turned, b, u, g_hi[:, s], late_upper, halves(turned.tile(u))[:, half],
                          gcn_scale[:, s:s + 1])

            def aggregate3(b, g):
                turned.wait_drained(ac, b, T_AGG3 + g)
                act(work[:, pair(g)], work[:, pair(g)], ACT.Tanh).then_inc(tanh_done.semaphore, 1)

            program(ac, "scalar", {
                "norm0": lambda b, _: normalise(norm0, b, h01, x1),
                "turn0": lambda b, t: upper(front, b, F_TURN0 + t, fT_hi[:, t], front_upper),
                "project0": project0,
                "norm1": lambda b, _: normalise(norm1, b, h01, x1), "split1": split1, "keep": keep,
                "edges1": lambda b, g: edges(b, g, F_EDGES1),
                "nodes1": lambda b, t: upper(front, b, F_NODES1 + t, fT_hi[:, t], front_upper),
                "expand1": expand1,
                "turn1": lambda b, t: upper(front, b, F_TURN1 + t, rT_hi[t], front_upper),
                "split2": split2,
                "edges2": lambda b, g: edges(b, g, F_EDGES2),
                "norm2": norm2_,
                "turn2": lambda b, t: upper(back, b, B_TURN2 + t, cT_hi[:, t], back_upper),
                "queries": lambda b, t: qk(b, B_QUERIES + t, 0, t, bq_col),
                "keys": lambda b, t: qk(b, B_KEYS + t, 1, t, bk_col),
                "scores": scores, "probs": probs,
                "turn_ctx": lambda b, t: upper(turned, b, T_TURN_CTX + t, cT_hi[:, t], late_upper,
                                               scale=1.0 / PROB_SCALE),
                "norm3": lambda b, _: normalise(norm3, b, work, x3),
                "turn3": lambda b, t: upper(turned, b, T_TURN3 + t, bT_hi[:, t], late_upper),
                "project3": project3, "aggregate3": aggregate3,
            })

        @block.gpsimd
        def _(gp):
            ng = nc.gpsimd
            ng.memset(ident[:], 0.0).then_inc(ident_zero, 1)
            gp.wait_ge(ident_zero, 1)
            ng.affine_select(out=ident[:], in_=ident[:], compare_op=ALU.not_equal, fill=1.0, base=0,
                             pattern=[[-1, P]], channel_multiplier=1).then_inc(ident_done, 1)
            ng.memset(mean_w, 1.0 / DH).then_inc(consts, 1)
            ng.memset(eps4[:], LN_EPS).then_inc(consts, 1)
            ng.memset(minus1[:], -1.0).then_inc(consts, 1)
            ng.memset(minus_half[:], -0.5).then_inc(consts, 1)
            ng.memset(proj[:, :, 2 * D:2 * D + 2], 1.0).then_inc(consts, 1)
            gp.wait_ge(consts, CONSTS)
            gp.wait_ge(ident_done, 1)
            gp.wait_ge(ready, READY)

            def scalars(norm, b):
                wait(gp, norm.mv_done, b, NTILE)
                ng.tensor_tensor(norm.var[:], norm.mv[:, :, 1], eps4[:], ALU.add).then_inc(norm.prep_done.semaphore, 1)
                ng.tensor_tensor(norm.neg[:], norm.mv[:, :, 0], minus1[:], ALU.mult).then_inc(
                    norm.prep_done.semaphore, 1)
                wait(gp, norm.prep_done, b, 2)
                ng.tensor_tensor(norm.rstd[:], norm.var[:], minus_half[:], ALU.pow).then_inc(
                    norm.rstd_done.semaphore, 1)
                wait(gp, norm.rstd_done, b, 1)
                ng.tensor_tensor(norm.shift[:], norm.neg[:], norm.rstd[:], ALU.mult).then_inc(
                    norm.shift_done.semaphore, 1)

            def split1(b, _):
                wait(gp, h1_upper, b, NTILE)
                ng.tensor_tensor(split_lo, h01[:], f32(split_hi), ALU.subtract).then_inc(h1_lower.semaphore, 1)
                ng.tensor_tensor(x1[:], x1[:], h01[:], ALU.add).then_inc(base1_half.semaphore, 1)
                wait(gp, base1_half, b, 1)
                ng.tensor_tensor(x1[:], x1[:], rows4(b2_rows, NTILE), ALU.add).then_inc(base1_done.semaphore, 1)

            def split2(b, _):
                wait(gp, p_upper, b, 1)
                ng.tensor_tensor(split_lo, h01[:], f32(split_hi), ALU.subtract).then_inc(p_lower.semaphore, 1)

            def keep(b, _):
                for k in range(2):
                    wait_for_earlier_batches(gp, turned.drained[k], b)
                wait(gp, gcn_degree_done, b, 1)
                ng.tensor_tensor(gcn_scale[:], gcn_degree[:], minus_half[:], ALU.pow).then_inc(
                    gcn_scale_done.semaphore, 1)
                wait(gp, norm2.done, b, NTILE)
                ng.tensor_tensor(x2[:], x2[:], rows4(bo_rows, NTILE), ALU.add).then_inc(base2_done.semaphore, 1)

            def value_parts(b, _):
                def heads(tensor):
                    return tensor[:].rearrange("p t (h d) -> p (t h) d", d=HD)

                parts = v_parts[:].rearrange("p t h c d -> p (t h) c d")
                wait(gp, v_part1, b, 1)
                ng.tensor_tensor(heads(ctx_n), heads(ctx_n), parts[:, :, 0], ALU.subtract).then_inc(v_rest1.semaphore, 1)
                wait(gp, v_part2, b, 1)
                ng.tensor_tensor(parts[:, :, 2], heads(ctx_n), parts[:, :, 1], ALU.subtract).then_inc(
                    v_part3.semaphore, 1)

            def aggregate3(b, g):
                wait(gp, tanh_done, b, g + 1)
                ng.tensor_tensor(x3[:, pair(g)], x3[:, pair(g)], work[:, pair(g)], ALU.add).then_inc(
                    result_done.semaphore, 1)

            program(gp, "gpsimd", {
                "norm0": lambda b, _: scalars(norm0, b), "norm1": lambda b, _: scalars(norm1, b),
                "norm_r": lambda b, _: scalars(norm_r, b), "norm2": lambda b, _: scalars(norm2, b),
                "norm3": lambda b, _: scalars(norm3, b),
                "split1": split1, "split2": split2, "keep": keep,
                "value_parts": value_parts, "aggregate3": aggregate3,
            })


def kernel(x, adj, L0_gnn_W, L1_gnn_W1, L1_gnn_b1, L1_gnn_gamma, L1_gnn_beta, L1_gnn_W2, L1_gnn_b2,
           L2_gnn_Wq, L2_gnn_bq, L2_gnn_Wk, L2_gnn_bk, L2_gnn_Wv, L2_gnn_bv, L2_gnn_Wo, L2_gnn_bo,
           L3_gnn_W, L3_gnn_b):
    import numpy as np
    import concourse.bacc as bacc
    from concourse.bass_utils import run_bass_kernel_spmd

    nc = bacc.Bacc("TRN2", target_bir_lowering=False, num_devices=1)

    def columns(a):
        return np.asarray(a).reshape(-1, P).T

    laid_out = [
        ("x", x), ("adj", adj), ("adjT", np.asarray(adj).transpose(0, 2, 1)),
        ("w0T", np.asarray(L0_gnn_W).T), ("w1T", np.asarray(L1_gnn_W1).T), ("b1", L1_gnn_b1),
        ("gamma", columns(L1_gnn_gamma)), ("beta", columns(L1_gnn_beta)), ("w2T", np.asarray(L1_gnn_W2).T), ("b2", L1_gnn_b2),
        ("wqT", np.asarray(L2_gnn_Wq).T), ("bq", columns(L2_gnn_bq)), ("wkT", np.asarray(L2_gnn_Wk).T), ("bk", columns(L2_gnn_bk)),
        ("wvT", np.asarray(L2_gnn_Wv).T), ("bv", L2_gnn_bv), ("woT", np.asarray(L2_gnn_Wo).T), ("bo", L2_gnn_bo),
        ("w3", L3_gnn_W), ("b3", L3_gnn_b),
    ]
    arrays, args = {}, []
    for name, a in laid_out:
        arrays[f"in_{name}"] = np.ascontiguousarray(a)
        args.append(nc.dram_tensor(f"in_{name}", arrays[f"in_{name}"].shape, F32, kind="ExternalInput").ap())
    out = nc.dram_tensor("out_x", np.asarray(x).shape, F32, kind="ExternalOutput").ap()
    gnn_stack(nc, *args, out)
    result = run_bass_kernel_spmd(nc, [arrays], core_ids=[0])
    return result.results[0]["out_x"]
```

```python
from contextlib import ExitStack

import concourse.bass as bass
from concourse import mybir

F32 = mybir.dt.float32
F32R = mybir.dt.float32r
F16 = mybir.dt.float16
BF16 = mybir.dt.bfloat16
ALU = mybir.AluOpType
ACT = mybir.ActivationFunctionType
AX_X = mybir.AxisListType.X

P = 128
DMA = 16
CONSTS = 5
LN_EPS = 1e-5
DEG_EPS = 1e-6
TINY = 1e-38
PROB_SCALE = 1024.0


class Signal:

    def __init__(self, semaphore, per_batch):
        self.semaphore, self.per_batch = semaphore, per_batch

    def after(self, b, n):
        return b * self.per_batch + n


def wait(eng, signal, b, n):
    eng.wait_ge(signal.semaphore, signal.after(b, n))


def wait_for_earlier_batches(eng, signal, b):
    if isinstance(b, int) and b == 0:
        return
    eng.wait_ge(signal.semaphore, signal.after(b, 0))


class Bank:

    def __init__(self, tiles, filled, drained):
        self.tiles, self.filled, self.drained = tiles, filled, drained

    def tile(self, u):
        return self.tiles[u % 2]

    def wait_free(self, eng, b, u):
        s = self.drained[u % 2]
        n = s.after(b, u // 2)
        if not (isinstance(n, int) and n == 0):
            eng.wait_ge(s.semaphore, n)

    def wait_read_out(self, eng, b, inputs, u):
        for k in range(2):
            uses = [v for v in (*inputs, u - 2) if v % 2 == k]
            if uses:
                self.wait_drained(eng, b, max(uses))

    def wait_filled(self, eng, b, u):
        eng.wait_ge(self.filled[u % 2].semaphore, self.filled[u % 2].after(b, u // 2 + 1))

    def wait_drained(self, eng, b, u):
        eng.wait_ge(self.drained[u % 2].semaphore, self.drained[u % 2].after(b, u // 2 + 1))

    def fill(self, instruction, u):
        instruction.then_inc(self.filled[u % 2].semaphore, 1)

    def drain(self, instruction, u):
        instruction.then_inc(self.drained[u % 2].semaphore, 1)


FRONT = (
    [("norm0", 0), ("masks", 0), ("apply0", 0), ("apply0", 1), ("masks", 1)]
    + [("turn0", 0), ("masks", 2), ("turn0", 1), ("masks", 3)]
    + [("project0", t) for t in range(4)]
    + [s for t in range(3) for s in (("edge_masks", t), ("aggregate0", t), ("update0", t))]
    + [("aggregate0", 3), ("update0", 3), ("norm1", 0), ("edge_masks", 3)]
    + [("apply1", 0), ("apply1", 1), ("split1", 0), ("split1", 1)]
    + [("edges1", g) for g in range(2)]
    + [("nodes1", t) for t in range(2)]
    + [("expand1", t) for t in range(4)]
    + [("norm_r", 0)]
    + [("turn1", t) for t in range(4)]
    + [("contract1", t) for t in range(4)]
    + [("edges2", g) for g in range(2)]
    + [("nodes2", g) for g in range(2)]
)
HEAD = [
    ("late", "norm3", 0), ("back", "norm2", 0),
    ("late", "turn3", 0), ("late", "turn3", 1), ("back", "turn2", 0), ("back", "turn2", 1),
    ("late", "project3", 0), ("late", "project3", 1), ("back", "queries", 0), ("back", "queries", 1),
    ("late", "aggregate3", 0), ("late", "aggregate3", 1), ("back", "keys", 0), ("back", "keys", 1),
    ("back", "keep", 0), ("back", "values", 0), ("back", "values", 1), ("back", "value_parts", 0),
    ("back", "base2", 0),
]
TAIL = [("back", "turn_ctx", 0), ("back", "turn_ctx", 1), ("back", "output2", 0), ("back", "output2", 1)]
GROUPS = {"late": -1, "back": 0, "front": 1}
NT = 32

PACE = {
    "tensor": [("scores", 1), ("context", -3), ("probs", -1)],
    "vector": [("scores", 0), ("probs", -2), ("weigh", -3)],
    "scalar": [("scores", 0), ("probs", -1)],
    "gpsimd": [],
}
BEFORE, AFTER = 1, 3

FRONT_SLOT = {
    "tensor": [
        0, 2, 2, 2, 2, 2, 2, 5, 8, 9, 11, 14, 16, 16, 20, 20, 21, 22, 26, 26, 26, 27, 27, 27, 28, 28, 28,
        28, 29, 30, 32, 33, 35, 38, 41, 42, 42, 43, 44, 45, 46, 47, 47, 48, 48, 49, 49, 51, 52, 56, 56],
    "vector": [
        0, 1, 3, 3, 3, 3, 5, 5, 10, 10, 13, 19, 19, 19, 21, 23, 24, 25, 27, 27, 27, 27, 27, 27, 28, 30, 30,
        30, 31, 31, 33, 34, 36, 40, 41, 42, 43, 44, 45, 45, 47, 47, 47, 48, 50, 50, 50, 53, 54, 55, 56],
    "scalar": [
        0, 0, 0, 0, 1, 2, 2, 5, 6, 8, 11, 16, 16, 16, 21, 21, 23, 23, 28, 28, 29, 29, 29, 29, 29, 29, 29,
        29, 29, 30, 32, 33, 35, 39, 42, 42, 44, 44, 45, 45, 46, 47, 47, 47, 49, 49, 49, 51, 52, 56, 56],
    "gpsimd": [
        0, 0, 0, 0, 0, 1, 5, 6, 7, 9, 11, 17, 17, 17, 24, 24, 24, 24, 27, 27, 27, 27, 29, 29, 29, 29, 32,
        32, 32, 32, 32, 32, 32, 34, 36, 36, 38, 40, 41, 43, 43, 43, 43, 44, 45, 45, 45, 46, 48, 53, 53],
}


def attention_step(t, pace):
    step = []
    for stage, ahead in pace:
        u = t + ahead
        if 0 <= u < NT and stage != "weigh":
            step.append(("back", stage, u))
        if 0 <= u < NT and stage == "weigh" and u % 4 == 3:
            step.append(("back", stage, u // 4))
    return step


def body(engine, groups):
    slots = ([[s] for s in HEAD]
             + [attention_step(t, PACE[engine]) for t in range(-BEFORE, NT + AFTER)]
             + [[s] for s in TAIL])
    slots[len(HEAD) + BEFORE].append(("back", "value_parts", 1))
    order, done = [], 0
    for i, slot in enumerate(slots):
        order += slot
        while done < len(FRONT) and (FRONT_SLOT[engine][done] <= i or i == len(slots) - 1):
            order.append(("front", *FRONT[done]))
            done += 1
    return [s for s in order if s[0] in groups]


F_TURN0, F_PROJECT0, F_AGG0, F_EDGES1, F_NODES1, F_EXPAND1, F_TURN1, F_CONTRACT1, F_EDGES2, F_NODES2 = (
    0, 2, 6, 10, 12, 14, 18, 22, 24, 26)
F_USES = 28
B_TURN2, B_QUERIES, B_KEYS, B_VALUES, B_SCORES = 0, 2, 4, 6, 8
B_USES = B_SCORES + NT
T_PROBS, T_TURN_CTX, T_OUTPUT2, T_TURN3, T_PROJECT3, T_AGG3 = 0, NT, NT + 2, NT + 4, NT + 6, NT + 8
T_USES = NT + 10


def gnn_stack(nc, x, adj, adjT, w0T, w1T, b1, gamma_cols, beta_cols, w2T, b2, wqT, bq_cols,
              wkT, bk_cols, wvT, bv, woT, bo,
              w3, b3, out):
    B, N, D = x.shape
    NTILE = N // P
    DT = D // P
    DH = w1T.shape[1]
    HT = DH // P
    HEADS = 8
    HD = D // HEADS
    PER_TILE = P // HD
    PARTS = 3
    SCORE_SCALE = 2.0 * HD ** -0.5
    assert N == 512 and D == 256 and DH == 512 and NT == NTILE * HEADS

    with ExitStack() as ctx:
        def sb(name, shape, dt=F32):
            return ctx.enter_context(nc.sbuf_tensor(name, shape, dt))

        def sem(name):
            return ctx.enter_context(nc.semaphore(name))

        def signal(name, per_batch=1):
            return Signal(sem(name), per_batch)

        def banks(name, uses):
            tiles = [ctx.enter_context(nc.psum_tensor(f"{name}{i}", [P, 512], F32)) for i in range(2)]
            return Bank(tiles, [signal(f"{name}_filled{i}", uses // 2) for i in range(2)],
                        [signal(f"{name}_drained{i}", uses // 2) for i in range(2)])

        front = banks("front", F_USES)
        back = banks("back", B_USES)
        turned = banks("turned", T_USES)
        mixed = banks("mixed", 8)

        ident = sb("ident", [P, P])
        eps4 = sb("eps4", [P, NTILE])
        minus1 = sb("minus1", [P, NTILE])
        minus_half = sb("minus_half", [P, NTILE])
        WIDTH = dict(w0=(DT, 2 * D), w1=(DT, DH), w2=(HT, D), wq=(DT, D), wk=(DT, D), wv=(DT, D), wo=(DT, D),
                     w3=(DT, D))
        w_hi = {n: sb(f"{n}_hi", [P, *s], F32R) for n, s in WIDTH.items()}
        w_lo = {n: sb(f"{n}_lo", [P, *s], F32R) for n, s in WIDTH.items()}
        b1_rows = sb("b1_rows", [P, DH])
        b2_rows, bv_rows, bo_rows, b3_rows = (sb(n, [P, D]) for n in ("b2_rows", "bv_rows", "bo_rows", "b3_rows"))
        bq_col, bk_col = sb("bq_col", [P, DT]), sb("bk_col", [P, DT])
        gamma_col, beta_col = sb("gamma_col", [P, HT]), sb("beta_col", [P, HT])
        shift2_rows = sb("shift2_rows", [P, D])

        def view(tensor, a, b):
            return tensor[:].rearrange("p t c -> p (t c)").rearrange("p (a b) -> p a b", a=a, b=b)

        x1 = sb("x1", [P, NTILE, D])
        adj_f = sb("adj_f", [P, NTILE, N])
        adjT_f = sb("adjT_f", [P, NTILE, N])
        edge_w = sb("edge_w", [P, N])
        h01 = sb("h01", [P, NTILE, D])
        proj = sb("proj", [P, NTILE, 2 * D + 2])
        r = proj[:, :, 0:DH]
        degree = sb("degree", [P, NTILE, 2])
        H = sb("H", [P, NTILE, N], F32R)
        HTr = sb("HTr", [P, NTILE, N], F32R)
        row_count = sb("row_count", [P, NTILE])
        edge_size = sb("edge_size", [P, NTILE])
        node_w = sb("node_w", [P, NTILE])
        diag = sb("diag", [P, NTILE])
        shift_weight = sb("shift_weight", [P, NTILE])
        edge_inv, node_inv = sb("edge_inv", [P, NTILE]), sb("node_inv", [P, NTILE])
        inv_tmp = sb("inv_tmp", [P, 2, NTILE])
        gcn_degree = sb("gcn_degree", [P, NTILE])
        fT_hi, fT_lo = sb("fT_hi", [P, DT, N], F32R), sb("fT_lo", [P, DT, N], F32R)
        m_hi, m_lo = sb("m_hi", [P, NTILE, D], F32R), sb("m_lo", [P, NTILE, D], F32R)
        scratch = view(m_lo, DT, N)
        split_hi, split_lo = view(fT_hi, NTILE, D), view(fT_lo, NTILE, D)
        rT_hi = [fT_hi[:, 0], fT_hi[:, 1], view(m_hi, DT, N)[:, 0], view(m_hi, DT, N)[:, 1]]
        rT_lo = [fT_lo[:, 0], fT_lo[:, 1], view(m_lo, DT, N)[:, 0], view(m_lo, DT, N)[:, 1]]

        x2 = sb("x2", [P, NTILE, D])
        adj_b = sb("adj_b", [P, NTILE, N])
        AT = sb("AT", [P, NTILE, N], F32R)
        gcn_scale = sb("gcn_scale", [P, NTILE])
        work = sb("work", [P, NTILE, D])
        bT_hi, bT_lo = sb("bT_hi", [P, DT, N], F32R), sb("bT_lo", [P, DT, N], F32R)
        g_hi, g_lo = sb("g_hi", [P, NTILE, D], F32R), sb("g_lo", [P, NTILE, D], F32R)
        cT_hi, cT_lo = sb("cT_hi", [P, DT, N], F32R), sb("cT_lo", [P, DT, N], F32R)
        ctx_n = sb("ctx_n", [P, NTILE, D])
        qk_hi = [bT_hi, view(g_hi, DT, N)]
        qk_lo = [bT_lo, view(g_lo, DT, N)]
        stacks = [sb("q_stack", [P, 2, DT, N], F32R), sb("k_stack", [P, 2, DT, N], F32R)]
        x3 = sb("x3", [P, NTILE, D])
        v_parts = sb("v_parts", [P, NTILE, HEADS, PARTS, HD], BF16)
        SLOTS = 3
        masked = sb("masked", [P, SLOTS, N])
        top, minus_top = sb("top", [P, NT]), sb("minus_top", [P, NT])
        prob_sum = sb("prob_sum", [P, NT])
        prob_inv = sb("prob_inv", [P, NT])
        probsT_hi, probsT_lo = sb("probsT_hi", [P, 2, N], F16), sb("probsT_lo", [P, 2, N], F16)

        def part_of(tensor, at, a, b):
            flat = tensor[:].rearrange("p t c -> p (t c)")
            return flat[:, at:at + a * b].rearrange("p (a b) -> p a b", a=a, b=b)

        raw = dict(w0=part_of(x3, 0, DT, 2 * D), w1=part_of(work, 0, DT, DH), w2=part_of(ctx_n, 0, HT, D),
                   wq=part_of(adj_b, 0, DT, D), wk=part_of(adj_b, 2 * D, DT, D), wv=part_of(adj_b, 4 * D, DT, D),
                   wo=part_of(adj_b, 6 * D, DT, D), w3=part_of(x2, 0, DT, D))
        mean_w = part_of(masked, HT * D, 1, P)[:, 0]
        w2g = part_of(masked, 0, HT, D)

        loaded = sem("loaded")
        ident_zero, ident_done, consts = sem("ident_zero"), sem("ident_done"), sem("consts")
        gamma_done, mean_done, shift_done, centred = (
            sem(n) for n in ("gamma_done", "mean_done", "shift_done", "centred"))
        wq_scaled, uppers = sem("wq_scaled"), sem("uppers")
        passed = sem("passed")
        ready = sem("ready")
        READY = len(WIDTH) + 2

        x_loaded, adjT_loaded, adj_loaded, edge_w_loaded, adj_b_loaded = (
            signal(n, DMA) for n in ("x_loaded", "adjT_loaded", "adj_loaded", "edge_w_loaded", "adj_b_loaded"))
        stored = signal("stored", DMA)
        PAIR_DMAS = 8
        stacked = [signal(f"stacked{i}", 2 * PAIR_DMAS * DMA) for i in range(2)]

        class Norm:

            def __init__(self, name):
                self.stats = sb(f"{name}_stats", [P, NTILE, 6])
                self.mv = sb(f"{name}_mv", [P, NTILE, 2])
                self.var = sb(f"{name}_var", [P, NTILE])
                self.neg = sb(f"{name}_neg", [P, NTILE])
                self.rstd = sb(f"{name}_rstd", [P, NTILE])
                self.shift = sb(f"{name}_shift", [P, NTILE])
                self.stats_done = signal(f"{name}_stats_done", NTILE)
                self.mv_done = signal(f"{name}_mv_done", NTILE)
                self.prep_done = signal(f"{name}_prep_done", 2)
                self.rstd_done = signal(f"{name}_rstd_done")
                self.shift_done = signal(f"{name}_shift_done")
                self.done = signal(f"{name}_done", NTILE)

        norm0, norm1, norm_r, norm2, norm3 = (Norm(n) for n in ("norm0", "norm1", "norm_r", "norm2", "norm3"))
        UPPER_TURN0, UPPER_EDGES1, UPPER_NODES1, UPPER_TURN1, UPPER_CONTRACT1, UPPER_EDGES2 = (
            0, 2, 6, 8, 12, 16)
        front_upper = signal("front_upper", 20)
        UPPER_TURN2, UPPER_QUERIES = 0, 2
        back_upper = signal("back_upper", 6)
        UPPER_TURN_CTX, UPPER_TURN3, UPPER_PROJECT3 = 0, 2, 4
        late_upper = signal("late_upper", 8)
        degree_floor, degree_inv = signal("degree_floor", NTILE), signal("degree_inv", NTILE)
        x1_done = signal("x1_done", NTILE)
        masks_done, edge_masks_done = signal("masks_done", 3 * NTILE), signal("edge_masks_done", NTILE)
        inv_floor, inv_recip, inv_done = signal("inv_floor", 2), signal("inv_recip"), signal("inv_done", 2)
        gcn_degree_done = signal("gcn_degree_done")
        h1_upper, h1_lower = signal("h1_upper", NTILE), signal("h1_lower", 2)
        base1_steps, shift_weight_done, base1_done = (
            signal("base1_steps", 3), signal("shift_weight_done"), signal("base1_done"))
        relu_done = signal("relu_done", NTILE)
        AT_copied, AT_done, gcn_scale_done = signal("AT_copied"), signal("AT_done", NTILE), signal("gcn_scale_done")
        v_part1, v_rest1, v_part2, v_part3 = (signal(n) for n in ("v_part1", "v_rest1", "v_part2", "v_part3"))
        neg_done, exp_done = signal("neg_done", NT), signal("exp_done", NT)
        probsT_upper = signal("probsT_upper", NT)
        context_done = signal("context_done", NT)
        prob_inv_done, ctx_done = signal("prob_inv_done", HEADS), signal("ctx_done", HEADS)
        base2_done = signal("base2_done")
        tanh_done, result_done = signal("tanh_done", 2), signal("result_done", 2)

        block = ctx.enter_context(nc.Block())

        WEIGHTS = [
            (raw["w1"], w1T.rearrange("(kt p) h -> p kt h", p=P)),
            (raw["w2"], w2T.rearrange("(kt p) o -> p kt o", p=P)),
            (raw["wq"], wqT.rearrange("(kt p) o -> p kt o", p=P)),
            (raw["wk"], wkT.rearrange("(kt p) o -> p kt o", p=P)),
            (raw["wv"], wvT.rearrange("(kt p) o -> p kt o", p=P)),
            (raw["wo"], woT.rearrange("(kt p) o -> p kt o", p=P)),
            (raw["w3"], w3.rearrange("(kt p) o -> p kt o", p=P)),
            (b1_rows, b1.partition_broadcast(P)),
            (b2_rows, b2.partition_broadcast(P)),
            (bv_rows, bv.partition_broadcast(P)),
            (bo_rows, bo.partition_broadcast(P)),
            (b3_rows, b3.partition_broadcast(P)),
            (bq_col, bq_cols),
            (bk_col, bk_cols),
            (gamma_col, gamma_cols),
            (beta_col, beta_cols),
        ]
        w0_v = w0T.rearrange("(half kt p) o -> p half kt o", half=2, p=P)
        LOADS = len(WEIGHTS) + 2
        x_v = x.rearrange("b (t p) f -> b p t f", p=P)
        out_v = out.rearrange("b (t p) f -> b p t f", p=P)
        adj_v = adj.rearrange("b (t p) j -> b p t j", p=P)
        adjT_v = adjT.rearrange("b (t p) j -> b p t j", p=P)

        def f32(ap):
            return ap.bitcast(F32)

        def wait_alone(eng, signal, b, n):
            wait(eng, signal, b, n)
            eng.sem_inc(passed, 1)

        def program(eng, engine, steps):

            def run(i, groups):
                for group, name, n in body(engine, groups):
                    if name in steps:
                        steps[name](i + GROUPS[group], n)

            run(-1, ["front"])
            run(0, ["back", "front"])
            with eng.Fori(1, B - 1) as i:
                run(i, ["late", "back", "front"])
            run(B - 1, ["late", "back"])
            run(B, ["late"])

        def cols(t):
            return slice(t * P, (t + 1) * P)

        def pair(g):
            return slice(2 * g, 2 * g + 2)

        def halves(tile):
            return tile[:].rearrange("p (t c) -> p t c", c=D)

        def rows4(rows, n):
            return rows[:].rearrange("p (o d) -> p o d", o=1).broadcast_to([P, n, D])

        def head_of(t):
            return (t // 4) % 2 * PER_TILE + t // 8

        @block.sync
        def _(sp):
            for half in range(2):
                sp.dma_start(raw["w0"][:, :, half * D:(half + 1) * D], w0_v[:, half]).then_inc(loaded, DMA)
            for dst, src in WEIGHTS:
                sp.dma_start(dst[:] if not isinstance(dst, bass.AP) else dst, src).then_inc(loaded, DMA)

            def load_front(b):
                for k in range(2):
                    wait_for_earlier_batches(sp, front.drained[k], b)
                sp.dma_start(x1[:], x_v[b]).then_inc(x_loaded.semaphore, DMA)
                wait_for_earlier_batches(sp, edge_masks_done, b)
                sp.dma_start(adjT_f[:], adjT_v[b]).then_inc(adjT_loaded.semaphore, DMA)
                wait_for_earlier_batches(sp, masks_done, b)
                sp.dma_start(adj_f[:], adj_v[b]).then_inc(adj_loaded.semaphore, DMA)
                sp.dma_start(edge_w[:], adj[b, 0].partition_broadcast(P)).then_inc(edge_w_loaded.semaphore, DMA)

            def load_back(b):
                if not (isinstance(b, int) and b == 0):
                    for t in (NT - 2, NT - 1):
                        back.wait_drained(sp, b - 1, B_SCORES + t)
                sp.dma_start(adj_b[:], adj_v[b]).then_inc(adj_b_loaded.semaphore, DMA)

            def stack(b, j):
                if j >= 2:
                    for t in (8 * (j - 1) - 2, 8 * (j - 1) - 1):
                        back.wait_drained(sp, b, B_SCORES + t)
                for which, groups, first in ((0, "hhll", B_QUERIES), (1, "hlhl", B_KEYS)):
                    if j == 0:
                        for t in range(DT):
                            back.wait_drained(sp, b, first + t)
                    for g, part in enumerate(groups):
                        src = (qk_hi if part == "h" else qk_lo)[which]
                        sp.dma_start(stacks[which][HD * g:HD * (g + 1), j % 2].bitcast(F32),
                                     src[HD * j:HD * (j + 1)].bitcast(F32)).then_inc(
                                         stacked[j % 2].semaphore, DMA)

            def store(b):
                wait(sp, result_done, b, 2)
                sp.dma_start(out_v[b], x3[:]).then_inc(stored.semaphore, DMA)

            def back_half(b):
                load_back(b)
                for j in range(PER_TILE):
                    stack(b, j)
                    if j == 0 and not (isinstance(b, int) and b == 0):
                        store(b - 1)

            load_front(0)
            sp.wait_ge(ready, READY)
            load_front(1)
            back_half(0)
            with sp.Fori(1, B - 1) as i:
                load_front(i + 1)
                back_half(i)
            back_half(B - 1)
            store(B - 1)
            wait(sp, stored, B - 1, DMA)

        @block.tensor
        def _(pe):
            def transpose_tiles(bank, b, u, source, t, count):
                tile = bank.tile(u)
                for s in range(count):
                    last = nc.tensor.transpose(tile[:, s * P:(s + 1) * P], source[:, s, t * P:(t + 1) * P], ident[:])
                bank.fill(last, u)

            def split_product(dst, terms):
                n = len(terms)
                for i, (lh, ll, rh, rl) in enumerate(terms):
                    nc.tensor.matmul(dst, lh, rh, start=(i == 0), stop=False)
                    nc.tensor.matmul(dst, lh, rl, start=False, stop=False)
                    last = nc.tensor.matmul(dst, ll, rh, start=False, stop=(i == n - 1))
                return last

            def mask_product(dst, terms):
                n = len(terms)
                for i, (a, hi, lo, mask_left) in enumerate(terms):
                    for k, part in enumerate((hi, lo)):
                        l, rr = (a, part) if mask_left else (part, a)
                        last = nc.tensor.matmul(dst, l, rr, start=(i == 0 and k == 0), stop=(i == n - 1 and k == 1))
                return last

            pe.wait_ge(ident_done, 1)
            pe.wait_ge(consts, CONSTS)
            pe.wait_ge(loaded, LOADS * DMA)
            pe.wait_ge(gamma_done, HT)
            for kt in range(HT):
                last = nc.tensor.matmul(front.tiles[0][:, 0:D], mean_w, w2g[:, kt, :],
                                        start=(kt == 0), stop=(kt == HT - 1))
            last.then_inc(mean_done, 1)
            for kt in range(HT):
                last = nc.tensor.matmul(front.tiles[1][:, 0:D], beta_col[:, kt:kt + 1].broadcast_to([P, P]),
                                        raw["w2"][:, kt, :], start=(kt == 0), stop=(kt == HT - 1))
            last.then_inc(shift_done, 1)
            pe.wait_ge(ready, READY)

            def turn0(b, t):
                wait(pe, norm0.done, b, NTILE)
                front.wait_free(pe, b, F_TURN0 + t)
                transpose_tiles(front, b, F_TURN0 + t, h01, t, NTILE)

            def project0(b, s):
                u = F_PROJECT0 + s
                front.wait_read_out(pe, b, [F_TURN0, F_TURN0 + 1] if s == 0 else [], u)
                last = split_product(front.tile(u)[:], [
                    (fT_hi[:, k, cols(s)], fT_lo[:, k, cols(s)], w_hi["w0"][:, k, :], w_lo["w0"][:, k, :])
                    for k in range(DT)])
                front.fill(last, u)

            def aggregate0(b, t):
                u = F_AGG0 + t
                if t == 0:
                    wait(pe, adjT_loaded, b, DMA)
                front.wait_read_out(pe, b, [F_PROJECT0 + s for s in range(NTILE)] if t == 0 else [], u)
                for k in range(NTILE):
                    last = nc.tensor.matmul(front.tile(u)[:, 0:D + 1], adjT_f[:, k, cols(t)],
                                            proj[:, k, D:2 * D + 1], start=(k == 0), stop=(k == NTILE - 1))
                front.fill(last, u)

            def gather(bank, b, u, matrix, hi, lo, g):
                for half in range(2):
                    last = mask_product(bank.tile(u)[:, half * D:(half + 1) * D], [
                        (matrix[:, k, cols(2 * g + half)], hi[:, k, :], lo[:, k, :], True) for k in range(NTILE)])
                bank.fill(last, u)

            def edges1(b, g):
                wait(pe, masks_done, b, 3 * NTILE)
                wait(pe, h1_upper, b, NTILE)
                wait(pe, h1_lower, b, 2)
                front.wait_free(pe, b, F_EDGES1 + g)
                gather(front, b, F_EDGES1 + g, H, split_hi, split_lo, g)

            def nodes1(b, t):
                u = F_NODES1 + t
                front.wait_read_out(pe, b, [F_EDGES1, F_EDGES1 + 1] if t == 0 else [], u)
                last = mask_product(front.tile(u)[:], [
                    (HTr[:, k, :], m_hi[:, k, cols(t)], m_lo[:, k, cols(t)], False) for k in range(NTILE)])
                front.fill(last, u)

            def expand1(b, s):
                u = F_EXPAND1 + s
                front.wait_read_out(pe, b, [F_NODES1, F_NODES1 + 1] if s == 0 else [], u)
                last = split_product(front.tile(u)[:], [
                    (fT_hi[:, k, cols(s)], fT_lo[:, k, cols(s)], w_hi["w1"][:, k, :], w_lo["w1"][:, k, :])
                    for k in range(DT)])
                front.fill(last, u)

            def turn1(b, t):
                wait(pe, relu_done, b, NTILE)
                front.wait_free(pe, b, F_TURN1 + t)
                transpose_tiles(front, b, F_TURN1 + t, r, t, NTILE)

            def contract1(b, s):
                g, half = s // 2, s % 2
                u = F_CONTRACT1 + g
                if half == 0:
                    front.wait_read_out(pe, b, [F_TURN1 + t for t in range(HT)] if g == 0 else [], u)
                last = split_product(front.tile(u)[:, half * D:(half + 1) * D], [
                    (rT_hi[k][:, cols(s)], rT_lo[k][:, cols(s)], w_hi["w2"][:, k, :], w_lo["w2"][:, k, :])
                    for k in range(HT)])
                if half == 1:
                    front.fill(last, u)

            def edges2(b, g):
                front.wait_read_out(pe, b, [F_CONTRACT1, F_CONTRACT1 + 1] if g == 0 else [], F_EDGES2 + g)
                gather(front, b, F_EDGES2 + g, H, split_hi, split_lo, g)

            def nodes2(b, g):
                front.wait_read_out(pe, b, [F_EDGES2, F_EDGES2 + 1] if g == 0 else [], F_NODES2 + g)
                gather(front, b, F_NODES2 + g, HTr, m_hi, m_lo, g)

            def turn2(b, t):
                wait(pe, norm2.done, b, NTILE)
                back.wait_free(pe, b, B_TURN2 + t)
                transpose_tiles(back, b, B_TURN2 + t, ctx_n, t, NTILE)

            def project_qk(b, u, name, t):
                back.wait_read_out(pe, b, [B_TURN2, B_TURN2 + 1], u)
                last = split_product(back.tile(u)[:], [
                    (w_hi[name][:, k, cols(t)], w_lo[name][:, k, cols(t)], cT_hi[:, k, :], cT_lo[:, k, :])
                    for k in range(DT)])
                back.fill(last, u)

            def project_rows(bank, b, u, hi, lo, name, g):
                for half in range(2):
                    s = 2 * g + half
                    last = split_product(bank.tile(u)[:, half * D:(half + 1) * D], [
                        (hi[:, k, cols(s)], lo[:, k, cols(s)], w_hi[name][:, k, :], w_lo[name][:, k, :])
                        for k in range(DT)])
                bank.fill(last, u)

            def values(b, g):
                back.wait_free(pe, b, B_VALUES + g)
                project_rows(back, b, B_VALUES + g, cT_hi, cT_lo, "wv", g)

            def scores(b, t):
                j, mt, qt = t // 8, t // 4 % 2, t % 4
                if t % 8 == 0:
                    wait(pe, stacked[j % 2], b, (j // 2 + 1) * PAIR_DMAS * DMA)
                u = B_SCORES + t
                back.wait_free(pe, b, u)
                back.fill(nc.tensor.matmul(back.tile(u)[:], stacks[0][:, j % 2, mt, cols(qt)],
                                           stacks[1][:, j % 2, mt, :], start=True, stop=True), u)

            def probs_turn(b, t):
                wait(pe, exp_done, b, t + 1)
                turned.wait_free(pe, b, t)
                for k in range(NTILE):
                    last = nc.tensor.transpose(turned.tile(t)[:, cols(k)], masked[:, t % SLOTS, cols(k)], ident[:])
                turned.fill(last, t)

            def context(b, t):
                if t == 0:
                    wait(pe, v_part1, b, 1)
                    wait(pe, v_part2, b, 1)
                    wait(pe, v_part3, b, 1)
                if t % 4 == 0:
                    mixed.wait_free(pe, b, t // 4)
                turned.wait_drained(pe, b, t)
                dst = mixed.tile(t // 4)[:, (t % 4) * PARTS * HD:(t % 4 + 1) * PARTS * HD]
                for k in range(NTILE):
                    v = v_parts[:, k, head_of(t)].rearrange("p c d -> p (c d)")
                    for part in (probsT_hi, probsT_lo):
                        last = nc.tensor.matmul(dst, part[:, t % 2, cols(k)], v,
                                                start=(k == 0 and part is probsT_hi),
                                                stop=(k == NTILE - 1 and part is probsT_lo))
                last.then_inc(context_done.semaphore, 1)

            def turn_ctx(b, t):
                wait(pe, ctx_done, b, HEADS)
                turned.wait_free(pe, b, T_TURN_CTX + t)
                transpose_tiles(turned, b, T_TURN_CTX + t, ctx_n, t, NTILE)

            def output2(b, g):
                turned.wait_read_out(pe, b, [T_TURN_CTX, T_TURN_CTX + 1] if g == 0 else [], T_OUTPUT2 + g)
                project_rows(turned, b, T_OUTPUT2 + g, cT_hi, cT_lo, "wo", g)

            def turn3(b, t):
                wait(pe, norm3.done, b, NTILE)
                turned.wait_free(pe, b, T_TURN3 + t)
                transpose_tiles(turned, b, T_TURN3 + t, work, t, NTILE)

            def project3(b, g):
                turned.wait_read_out(pe, b, [T_TURN3, T_TURN3 + 1] if g == 0 else [], T_PROJECT3 + g)
                project_rows(turned, b, T_PROJECT3 + g, bT_hi, bT_lo, "w3", g)

            def aggregate3(b, g):
                wait(pe, AT_done, b, NTILE)
                turned.wait_read_out(pe, b, [T_PROJECT3, T_PROJECT3 + 1] if g == 0 else [], T_AGG3 + g)
                gather(turned, b, T_AGG3 + g, AT, g_hi, g_lo, g)

            program(pe, "tensor", {
                "turn0": turn0, "project0": project0, "aggregate0": aggregate0,
                "edges1": edges1, "nodes1": nodes1, "expand1": expand1, "turn1": turn1,
                "contract1": contract1, "edges2": edges2, "nodes2": nodes2,
                "turn2": turn2,
                "queries": lambda b, t: project_qk(b, B_QUERIES + t, "wq", t),
                "keys": lambda b, t: project_qk(b, B_KEYS + t, "wk", t),
                "values": values,
                "scores": scores, "probs": probs_turn, "context": context,
                "turn_ctx": turn_ctx, "output2": output2,
                "turn3": turn3, "project3": project3, "aggregate3": aggregate3,
            })

        @block.vector
        def _(ve):
            nv = nc.vector

            ve.wait_ge(loaded, LOADS * DMA)
            for k in range(HT):
                nv.tensor_scalar(w2g[:, k], raw["w2"][:, k], gamma_col[:, k:k + 1], None, ALU.mult).then_inc(
                    gamma_done, 1)
            others = [n for n in WIDTH if n != "w2"]
            nv.tensor_scalar(raw["wq"], raw["wq"], SCORE_SCALE, None, ALU.mult).then_inc(wq_scaled, 1)
            ve.wait_ge(wq_scaled, 1)
            for n in others:
                nv.tensor_copy(w_hi[n][:], raw[n]).then_inc(uppers, 1)
            nv.tensor_scalar(bq_col[:], bq_col[:], SCORE_SCALE, None, ALU.mult).then_inc(ready, 1)
            ve.wait_ge(uppers, len(others))
            for n in others:
                nv.tensor_tensor(w_lo[n][:], raw[n], f32(w_hi[n][:]), ALU.subtract).then_inc(ready, 1)
            ve.wait_ge(gamma_done, HT)
            ve.wait_ge(mean_done, 1)
            for k in range(HT):
                nv.tensor_tensor(w2g[:, k], w2g[:, k], front.tiles[0][:, 0:D], ALU.subtract).then_inc(centred, 1)
            ve.wait_ge(centred, HT)
            nv.tensor_copy(w_hi["w2"][:], w2g).then_inc(uppers, 1)
            ve.wait_ge(uppers, len(others) + 1)
            nv.tensor_tensor(w_lo["w2"][:], w2g, f32(w_hi["w2"][:]), ALU.subtract).then_inc(ready, 1)
            ve.wait_ge(shift_done, 1)
            nv.tensor_copy(shift2_rows[:], front.tiles[1][:, 0:D]).then_inc(ready, 1)
            ve.wait_ge(consts, CONSTS)
            ve.wait_ge(ident_done, 1)

            def statistics(norm, b, source):
                for t in range(NTILE):
                    nv.bn_stats(norm.stats[:, t], source[:, t]).then_inc(norm.stats_done.semaphore, 1)
                mean_and_variance(norm, b)

            def mean_and_variance(norm, b):
                wait_alone(ve, norm.stats_done, b, NTILE)
                for t in range(NTILE):
                    nv.bn_aggr(norm.mv[:, t], norm.stats[:, t]).then_inc(norm.mv_done.semaphore, 1)

            def lower(bank, b, u, upper, n, dst, hi, source=None, scale=None):
                wait(ve, upper, b, n)
                source = bank.tile(u)[:] if source is None else source
                if scale is None:
                    return nv.tensor_tensor(dst, source, f32(hi), ALU.subtract)
                return nv.scalar_tensor_tensor(dst, source, scale, f32(hi), ALU.mult, ALU.subtract)

            def norm0_(b, _):
                wait(ve, x_loaded, b, DMA)
                statistics(norm0, b, x1)

            def turn0(b, t):
                u = F_TURN0 + t
                front.drain(lower(front, b, u, front_upper, UPPER_TURN0 + t + 1, fT_lo[:, t], fT_hi[:, t]), u)

            def aggregate0(b, t):
                u = F_AGG0 + t
                tile = front.tile(u)
                front.wait_filled(ve, b, u)
                nv.tensor_scalar(degree[:, t, 0:1], tile[:, D:D + 1], DEG_EPS, None, ALU.max).then_inc(
                    degree_floor.semaphore, 1)
                wait(ve, degree_floor, b, t + 1)
                nv.reciprocal(degree[:, t, 1:2], degree[:, t, 0:1]).then_inc(degree_inv.semaphore, 1)
                wait(ve, degree_inv, b, t + 1)
                front.drain(nv.scalar_tensor_tensor(h01[:, t], tile[:, 0:D], degree[:, t, 1:2], proj[:, t, 0:D],
                                                    ALU.mult, ALU.add), u)

            def update0(b, t):
                front.wait_drained(ve, b, F_AGG0 + t)
                nv.scalar_tensor_tensor(x1[:, t], h01[:, t], 0.0, x1[:, t], ALU.max, ALU.add).then_inc(
                    x1_done.semaphore, 1)
                wait(ve, x1_done, b, t + 1)
                nv.bn_stats(norm1.stats[:, t], x1[:, t]).then_inc(norm1.stats_done.semaphore, 1)

            def masks(b, t):
                if t == 0:
                    wait(ve, adj_loaded, b, DMA)
                    wait(ve, edge_w_loaded, b, DMA)
                nv.tensor_scalar(H[:, t], adj_f[:, t], 0.0, 0.0, ALU.not_equal, ALU.add,
                                 accum_out=row_count[:, t:t + 1]).then_inc(masks_done.semaphore, 1)
                if t > 0:
                    wait(ve, masks_done, b, 3 * t)
                nv.scalar_tensor_tensor(scratch[:, 0], adj_f[:, t], 0.0, edge_w[:], ALU.not_equal, ALU.mult,
                                        accum_out=node_w[:, t:t + 1]).then_inc(masks_done.semaphore, 1)
                nv.scalar_tensor_tensor(scratch[:, 1, 0:P], adj_f[:, t, cols(t)], 0.0, ident[:], ALU.not_equal,
                                        ALU.mult, accum_out=diag[:, t:t + 1]).then_inc(masks_done.semaphore, 1)

            def edge_masks(b, t):
                if t == 0:
                    wait_for_earlier_batches(ve, AT_copied, b)
                    wait(ve, adjT_loaded, b, DMA)
                nv.tensor_scalar(HTr[:, t], adjT_f[:, t], 0.0, 0.0, ALU.not_equal, ALU.add,
                                 accum_out=edge_size[:, t:t + 1]).then_inc(edge_masks_done.semaphore, 1)
                if t == NTILE - 1:
                    inverses(b)

            def inverses(b):
                wait(ve, masks_done, b, 3 * NTILE)
                wait(ve, edge_masks_done, b, NTILE)
                nv.tensor_scalar(inv_tmp[:, 0], edge_size[:], 1.0, None, ALU.max).then_inc(inv_floor.semaphore, 1)
                nv.tensor_scalar(inv_tmp[:, 1], node_w[:], TINY, None, ALU.max).then_inc(inv_floor.semaphore, 1)
                wait(ve, inv_floor, b, 2)
                nv.reciprocal(inv_tmp[:], inv_tmp[:]).then_inc(inv_recip.semaphore, 1)
                wait(ve, inv_recip, b, 1)
                nv.scalar_tensor_tensor(edge_inv[:], edge_size[:], 0.0, inv_tmp[:, 0], ALU.is_gt, ALU.mult).then_inc(
                    inv_done.semaphore, 1)
                nv.scalar_tensor_tensor(node_inv[:], node_w[:], 0.0, inv_tmp[:, 1], ALU.is_gt, ALU.mult).then_inc(
                    inv_done.semaphore, 1)
                wait_for_earlier_batches(ve, gcn_scale_done, b)
                nv.scalar_tensor_tensor(gcn_degree[:], row_count[:], 1.0, diag[:], ALU.add, ALU.subtract).then_inc(
                    gcn_degree_done.semaphore, 1)

            def norm1_(b, _):
                mean_and_variance(norm1, b)

            def edges(b, g, first_use, first_upper):
                u = first_use + g
                for half in range(2):
                    e = 2 * g + half
                    last = lower(front, b, u, front_upper, first_upper + 2 * g + 2, m_lo[:, e], m_hi[:, e],
                                 halves(front.tile(u))[:, half], edge_inv[:, e:e + 1])
                front.drain(last, u)

            def nodes1(b, t):
                u = F_NODES1 + t
                front.drain(lower(front, b, u, front_upper, UPPER_NODES1 + t + 1, fT_lo[:, t], fT_hi[:, t]), u)

            def expand1(b, s):
                u = F_EXPAND1 + s
                front.wait_filled(ve, b, u)
                front.drain(nv.scalar_tensor_tensor(r[:, s], front.tile(u)[:], node_inv[:, s:s + 1], b1_rows[:],
                                                    ALU.mult, ALU.add), u)

            def norm_r_(b, _):
                wait(ve, relu_done, b, NTILE)
                statistics(norm_r, b, r)

            def turn1(b, t):
                u = F_TURN1 + t
                front.drain(lower(front, b, u, front_upper, UPPER_TURN1 + t + 1, rT_lo[t], rT_hi[t]), u)

            def contract1(b, s):
                if s % 2 == 0:
                    return
                g = s // 2
                u = F_CONTRACT1 + g
                for half in range(2):
                    k = 2 * g + half
                    last = lower(front, b, u, front_upper, UPPER_CONTRACT1 + 2 * g + 2, split_lo[:, k],
                                 split_hi[:, k], halves(front.tile(u))[:, half], norm_r.rstd[:, k:k + 1])
                front.drain(last, u)

            def nodes2(b, g):
                u = F_NODES2 + g
                if g == 0 and not (isinstance(b, int) and b == 0):
                    wait(ve, base2_done, b - 1, 1)
                if g == 0:
                    wait(ve, base1_done, b, 1)
                front.wait_filled(ve, b, u)
                for half in range(2):
                    s = 2 * g + half
                    last = nv.scalar_tensor_tensor(x2[:, s], halves(front.tile(u))[:, half], node_inv[:, s:s + 1],
                                                   x1[:, s], ALU.mult, ALU.add)
                front.drain(last, u)

            def norm2_(b, _):
                for g in range(2):
                    front.wait_drained(ve, b, F_NODES2 + g)
                statistics(norm2, b, x2)

            def keep(b, _):
                wait(ve, AT_copied, b, 1)
                for t in range(NTILE):
                    nv.tensor_tensor(AT[:, t, cols(t)], f32(AT[:, t, cols(t)]), ident[:], ALU.max).then_inc(
                        AT_done.semaphore, 1)

            def turn_lower(bank, upper, b, t, first_use, first_upper, dst_lo, dst_hi, scale=None):
                u = first_use + t
                bank.drain(lower(bank, b, u, upper, first_upper + t + 1, dst_lo[:, t], dst_hi[:, t],
                                 scale=scale), u)

            def qk_lower(b, u, which, t, bias):
                wait(ve, back_upper, b, UPPER_QUERIES + u - B_QUERIES + 1)
                back.drain(nv.scalar_tensor_tensor(qk_lo[which][:, t], back.tile(u)[:], bias[:, t:t + 1],
                                                   f32(qk_hi[which][:, t]), ALU.add, ALU.subtract), u)

            def values(b, g):
                u = B_VALUES + g
                back.wait_filled(ve, b, u)
                back.drain(nv.tensor_tensor(ctx_n[:, pair(g)], halves(back.tile(u)), rows4(bv_rows, 2), ALU.add), u)

            def value_parts(b, n):
                if n == 1:
                    wait(ve, v_rest1, b, 1)
                    nv.tensor_copy(v_parts[:, :, :, 1], ctx_n[:].rearrange("p t (h d) -> p t h d", d=HD)).then_inc(
                        v_part2.semaphore, 1)
                    return
                for g in range(2):
                    back.wait_drained(ve, b, B_VALUES + g)
                wait_for_earlier_batches(ve, context_done, b)
                nv.tensor_copy(v_parts[:, :, :, 0], ctx_n[:].rearrange("p t (h d) -> p t h d", d=HD)).then_inc(
                    v_part1.semaphore, 1)

            def scores(b, t):
                u = B_SCORES + t
                if t == 0:
                    wait(ve, adj_b_loaded, b, DMA)
                if t >= SLOTS:
                    turned.wait_filled(ve, b, t - SLOTS)
                back.wait_filled(ve, b, u)
                ve.sem_inc(passed, 1)
                back.drain(nv.tensor_tensor_reduce(out=masked[:, t % SLOTS], in0=back.tile(u)[:],
                                                   in1=adj_b[:, t % 4], scale=1.0, scalar=-3e38, op0=ALU.mult,
                                                   op1=ALU.max, accum_out=top[:, t:t + 1]), u)

            def probs(b, t):
                wait(ve, probsT_upper, b, t + 1)
                turned.drain(nv.scalar_tensor_tensor(probsT_lo[:, t % 2], turned.tile(t)[:], PROB_SCALE,
                                                     probsT_hi[:, t % 2], ALU.mult, ALU.subtract), t)

            def weigh(b, h):
                wait(ve, context_done, b, 4 * (h + 1))
                head = head_of(4 * h)
                dst = ctx_n[:, :, head * HD:(head + 1) * HD]
                src = mixed.tile(h)[:, 0:NTILE * PARTS * HD].rearrange("p (q c d) -> p q d c", q=NTILE, c=PARTS)
                mixed.drain(nv.tensor_reduce(dst, src, AX_X, ALU.add), h)
                wait(ve, exp_done, b, 4 * (h + 1))
                nv.reciprocal(prob_inv[:, 4 * h:4 * h + 4], prob_sum[:, 4 * h:4 * h + 4]).then_inc(
                    prob_inv_done.semaphore, 1)
                mixed.wait_drained(ve, b, h)
                wait(ve, prob_inv_done, b, h + 1)
                inv = prob_inv[:, 4 * h:4 * h + 4].rearrange("p (q o) -> p q o", o=1).broadcast_to([P, NTILE, HD])
                nv.tensor_tensor(dst, dst, inv, ALU.mult).then_inc(ctx_done.semaphore, 1)

            def output2(b, g):
                u = T_OUTPUT2 + g
                wait(ve, base2_done, b, 1)
                turned.wait_filled(ve, b, u)
                turned.drain(nv.tensor_tensor(x3[:, pair(g)], halves(turned.tile(u)), x3[:, pair(g)], ALU.add), u)

            def norm3_(b, _):
                for g in range(2):
                    turned.wait_drained(ve, b, T_OUTPUT2 + g)
                statistics(norm3, b, x3)

            def project3(b, g):
                u = T_PROJECT3 + g
                for half in range(2):
                    s = 2 * g + half
                    last = lower(turned, b, u, late_upper, UPPER_PROJECT3 + 2 * g + 2, g_lo[:, s], g_hi[:, s],
                                 halves(turned.tile(u))[:, half], gcn_scale[:, s:s + 1])
                turned.drain(last, u)

            def aggregate3(b, g):
                u = T_AGG3 + g
                turned.wait_filled(ve, b, u)
                for half in range(2):
                    s = 2 * g + half
                    last = nv.scalar_tensor_tensor(work[:, s], halves(turned.tile(u))[:, half],
                                                   gcn_scale[:, s:s + 1], b3_rows[:], ALU.mult, ALU.add)
                turned.drain(last, u)

            program(ve, "vector", {
                "norm0": norm0_, "turn0": turn0, "aggregate0": aggregate0, "update0": update0,
                "masks": masks, "edge_masks": edge_masks, "norm1": norm1_,
                "edges1": lambda b, g: edges(b, g, F_EDGES1, UPPER_EDGES1), "nodes1": nodes1,
                "expand1": expand1, "norm_r": norm_r_, "turn1": turn1, "contract1": contract1,
                "edges2": lambda b, g: edges(b, g, F_EDGES2, UPPER_EDGES2), "nodes2": nodes2,
                "norm2": norm2_, "keep": keep,
                "turn2": lambda b, t: turn_lower(back, back_upper, b, t, B_TURN2, UPPER_TURN2, cT_lo, cT_hi),
                "queries": lambda b, t: qk_lower(b, B_QUERIES + t, 0, t, bq_col),
                "keys": lambda b, t: qk_lower(b, B_KEYS + t, 1, t, bk_col),
                "values": values, "value_parts": value_parts, "scores": scores, "probs": probs, "weigh": weigh,
                "turn_ctx": lambda b, t: turn_lower(turned, late_upper, b, t, T_TURN_CTX, UPPER_TURN_CTX,
                                                    cT_lo, cT_hi, 1.0 / PROB_SCALE),
                "output2": output2, "norm3": norm3_,
                "turn3": lambda b, t: turn_lower(turned, late_upper, b, t, T_TURN3, UPPER_TURN3, bT_lo, bT_hi),
                "project3": project3, "aggregate3": aggregate3,
            })

        @block.scalar
        def _(ac):
            act = nc.scalar.activation
            ac.wait_ge(ready, READY)
            ac.wait_ge(consts, CONSTS)

            def normalise(norm, b, dst, source, tiles=range(NTILE)):
                wait(ac, norm.rstd_done, b, 1)
                wait(ac, norm.shift_done, b, 1)
                for t in tiles:
                    act(dst[:, t], source[:, t], ACT.Relu, bias=norm.shift[:, t:t + 1],
                        scale=norm.rstd[:, t:t + 1]).then_inc(norm.done.semaphore, 1)

            def upper(bank, b, u, dst, signal, source=None, scale=1.0):
                bank.wait_filled(ac, b, u)
                act(dst, bank.tile(u)[:] if source is None else source, ACT.Copy,
                    scale=scale).then_inc(signal.semaphore, 1)

            def project0(b, s):
                u = F_PROJECT0 + s
                front.wait_filled(ac, b, u)
                front.drain(act(proj[:, s, 0:2 * D], front.tile(u)[:], ACT.Copy), u)

            def edges(b, g, first_use):
                wait(ac, inv_done, b, 2)
                u = first_use + g
                for half in range(2):
                    e = 2 * g + half
                    upper(front, b, u, m_hi[:, e], front_upper, halves(front.tile(u))[:, half],
                          edge_inv[:, e:e + 1])

            def expand1(b, s):
                front.wait_drained(ac, b, F_EXPAND1 + s)
                act(r[:, s], r[:, s], ACT.Relu).then_inc(relu_done.semaphore, 1)

            def contract1(b, s):
                if s % 2 == 0:
                    return
                g = s // 2
                if g == 0:
                    wait(ac, norm_r.rstd_done, b, 1)
                    front.wait_filled(ac, b, F_CONTRACT1 + 1)
                u = F_CONTRACT1 + g
                for half in range(2):
                    k = 2 * g + half
                    upper(front, b, u, split_hi[:, k], front_upper, halves(front.tile(u))[:, half],
                          norm_r.rstd[:, k:k + 1])

            def keep(b, _):
                wait(ac, edge_masks_done, b, NTILE)
                act(AT[:], f32(HTr[:]), ACT.Copy).then_inc(AT_copied.semaphore, 1)

            def split1(b, g):
                for t in range(2 * g, 2 * g + 2):
                    wait(ac, norm1.done, b, t + 1)
                    act(split_hi[:, t], h01[:, t], ACT.Copy).then_inc(h1_upper.semaphore, 1)

            def norm2_(b, _):
                normalise(norm2, b, ctx_n, x2)

            def qk(b, u, which, t, bias):
                back.wait_filled(ac, b, u)
                act(qk_hi[which][:, t], back.tile(u)[:], ACT.Identity,
                    bias=bias[:, t:t + 1]).then_inc(back_upper.semaphore, 1)

            def scores(b, t):
                back.wait_drained(ac, b, B_SCORES + t)
                act(minus_top[:, t:t + 1], top[:, t:t + 1], ACT.Copy, scale=-1.0).then_inc(neg_done.semaphore, 1)
                wait(ac, neg_done, b, t + 1)
                act(masked[:, t % SLOTS], masked[:, t % SLOTS], ACT.Exp, bias=minus_top[:, t:t + 1],
                    accum_out=prob_sum[:, t:t + 1]).then_inc(exp_done.semaphore, 1)

            def probs(b, t):
                if not (isinstance(b, int) and b == 0 and t < 2):
                    wait(ac, context_done, b, max(t - 1, 0))
                turned.wait_filled(ac, b, t)
                act(probsT_hi[:, t % 2], turned.tile(t)[:], ACT.Copy, scale=PROB_SCALE).then_inc(
                    probsT_upper.semaphore, 1)

            def project3(b, g):
                wait(ac, gcn_scale_done, b, 1)
                u = T_PROJECT3 + g
                for half in range(2):
                    s = 2 * g + half
                    upper(turned, b, u, g_hi[:, s], late_upper, halves(turned.tile(u))[:, half],
                          gcn_scale[:, s:s + 1])

            def aggregate3(b, g):
                turned.wait_drained(ac, b, T_AGG3 + g)
                act(work[:, pair(g)], work[:, pair(g)], ACT.Tanh).then_inc(tanh_done.semaphore, 1)

            program(ac, "scalar", {
                "apply0": lambda b, g: normalise(norm0, b, h01, x1, range(2 * g, 2 * g + 2)),
                "turn0": lambda b, t: upper(front, b, F_TURN0 + t, fT_hi[:, t], front_upper),
                "project0": project0,
                "apply1": lambda b, g: normalise(norm1, b, h01, x1, range(2 * g, 2 * g + 2)),
                "split1": split1, "keep": keep,
                "edges1": lambda b, g: edges(b, g, F_EDGES1),
                "nodes1": lambda b, t: upper(front, b, F_NODES1 + t, fT_hi[:, t], front_upper),
                "expand1": expand1,
                "turn1": lambda b, t: upper(front, b, F_TURN1 + t, rT_hi[t], front_upper),
                "contract1": contract1,
                "edges2": lambda b, g: edges(b, g, F_EDGES2),
                "norm2": norm2_,
                "turn2": lambda b, t: upper(back, b, B_TURN2 + t, cT_hi[:, t], back_upper),
                "queries": lambda b, t: qk(b, B_QUERIES + t, 0, t, bq_col),
                "keys": lambda b, t: qk(b, B_KEYS + t, 1, t, bk_col),
                "scores": scores, "probs": probs,
                "turn_ctx": lambda b, t: upper(turned, b, T_TURN_CTX + t, cT_hi[:, t], late_upper,
                                               scale=1.0 / PROB_SCALE),
                "norm3": lambda b, _: normalise(norm3, b, work, x3),
                "turn3": lambda b, t: upper(turned, b, T_TURN3 + t, bT_hi[:, t], late_upper),
                "project3": project3, "aggregate3": aggregate3,
            })

        @block.gpsimd
        def _(gp):
            ng = nc.gpsimd
            ng.memset(ident[:], 0.0).then_inc(ident_zero, 1)
            gp.wait_ge(ident_zero, 1)
            ng.affine_select(out=ident[:], in_=ident[:], compare_op=ALU.not_equal, fill=1.0, base=0,
                             pattern=[[-1, P]], channel_multiplier=1).then_inc(ident_done, 1)
            ng.memset(mean_w, 1.0 / DH).then_inc(consts, 1)
            ng.memset(eps4[:], LN_EPS).then_inc(consts, 1)
            ng.memset(minus1[:], -1.0).then_inc(consts, 1)
            ng.memset(minus_half[:], -0.5).then_inc(consts, 1)
            ng.memset(proj[:, :, 2 * D:2 * D + 2], 1.0).then_inc(consts, 1)
            gp.wait_ge(consts, CONSTS)
            gp.wait_ge(ident_done, 1)
            gp.wait_ge(ready, READY)

            def scalars(norm, b):
                wait(gp, norm.mv_done, b, NTILE)
                ng.tensor_tensor(norm.var[:], norm.mv[:, :, 1], eps4[:], ALU.add).then_inc(
                    norm.prep_done.semaphore, 1)
                ng.tensor_tensor(norm.neg[:], norm.mv[:, :, 0], minus1[:], ALU.mult).then_inc(
                    norm.prep_done.semaphore, 1)
                wait(gp, norm.prep_done, b, 2)
                ng.tensor_tensor(norm.rstd[:], norm.var[:], minus_half[:], ALU.pow).then_inc(
                    norm.rstd_done.semaphore, 1)
                wait(gp, norm.rstd_done, b, 1)
                ng.tensor_tensor(norm.shift[:], norm.neg[:], norm.rstd[:], ALU.mult).then_inc(
                    norm.shift_done.semaphore, 1)

            def split1(b, g):
                wait(gp, h1_upper, b, 2 * g + 2)
                ng.tensor_tensor(split_lo[:, pair(g)], h01[:, pair(g)], f32(split_hi[:, pair(g)]),
                                 ALU.subtract).then_inc(h1_lower.semaphore, 1)

            def base1(b, _):
                ng.tensor_tensor(x1[:], x1[:], h01[:], ALU.add).then_inc(base1_steps.semaphore, 1)
                wait(gp, base1_steps, b, 1)
                ng.tensor_tensor(x1[:], x1[:], rows4(b2_rows, NTILE), ALU.add).then_inc(base1_steps.semaphore, 1)
                wait(gp, inv_done, b, 2)
                ng.tensor_tensor(shift_weight[:], row_count[:], node_inv[:], ALU.mult).then_inc(
                    shift_weight_done.semaphore, 1)
                wait(gp, shift_weight_done, b, 1)
                weight = shift_weight[:].rearrange("p (t o) -> p t o", o=1).broadcast_to([P, NTILE, D])
                ng.tensor_tensor(h01[:], weight, rows4(shift2_rows, NTILE), ALU.mult).then_inc(
                    base1_steps.semaphore, 1)
                wait(gp, base1_steps, b, 3)
                ng.tensor_tensor(x1[:], x1[:], h01[:], ALU.add).then_inc(base1_done.semaphore, 1)

            def keep(b, _):
                for k in range(2):
                    wait_for_earlier_batches(gp, turned.drained[k], b)
                wait(gp, gcn_degree_done, b, 1)
                ng.tensor_tensor(gcn_scale[:], gcn_degree[:], minus_half[:], ALU.pow).then_inc(
                    gcn_scale_done.semaphore, 1)

            def base2(b, _):
                wait_for_earlier_batches(gp, stored, b)
                wait(gp, norm2.done, b, NTILE)
                ng.tensor_tensor(x3[:], x2[:], rows4(bo_rows, NTILE), ALU.add).then_inc(base2_done.semaphore, 1)

            def value_parts(b, n):
                def heads(tensor):
                    return tensor[:].rearrange("p t (h d) -> p (t h) d", d=HD)

                parts = v_parts[:].rearrange("p t h c d -> p (t h) c d")
                if n == 0:
                    wait(gp, v_part1, b, 1)
                    ng.tensor_tensor(heads(ctx_n), heads(ctx_n), parts[:, :, 0], ALU.subtract).then_inc(
                        v_rest1.semaphore, 1)
                    return
                wait(gp, v_part2, b, 1)
                ng.tensor_tensor(parts[:, :, 2], heads(ctx_n), parts[:, :, 1], ALU.subtract).then_inc(
                    v_part3.semaphore, 1)

            def aggregate3(b, g):
                wait(gp, tanh_done, b, g + 1)
                ng.tensor_tensor(x3[:, pair(g)], x3[:, pair(g)], work[:, pair(g)], ALU.add).then_inc(
                    result_done.semaphore, 1)

            program(gp, "gpsimd", {
                "norm0": lambda b, _: scalars(norm0, b), "norm1": lambda b, _: scalars(norm1, b),
                "norm_r": lambda b, _: scalars(norm_r, b), "norm2": lambda b, _: scalars(norm2, b),
                "norm3": lambda b, _: scalars(norm3, b),
                "split1": split1, "edges1": lambda b, g: base1(b, g) if g == 1 else None, "keep": keep,
                "base2": base2, "aggregate3": aggregate3,
                "value_parts": value_parts,
            })


def kernel(x, adj, L0_gnn_W, L1_gnn_W1, L1_gnn_b1, L1_gnn_gamma, L1_gnn_beta, L1_gnn_W2, L1_gnn_b2,
           L2_gnn_Wq, L2_gnn_bq, L2_gnn_Wk, L2_gnn_bk, L2_gnn_Wv, L2_gnn_bv, L2_gnn_Wo, L2_gnn_bo,
           L3_gnn_W, L3_gnn_b):
    import numpy as np
    import concourse.bacc as bacc
    from concourse.bass_utils import run_bass_kernel_spmd

    nc = bacc.Bacc("TRN2", target_bir_lowering=False, num_devices=1)

    def columns(a):
        return np.asarray(a).reshape(-1, P).T

    laid_out = [
        ("x", x), ("adj", adj), ("adjT", np.asarray(adj).transpose(0, 2, 1)),
        ("w0T", np.asarray(L0_gnn_W).T), ("w1T", np.asarray(L1_gnn_W1).T), ("b1", L1_gnn_b1),
        ("gamma", columns(L1_gnn_gamma)), ("beta", columns(L1_gnn_beta)), ("w2T", np.asarray(L1_gnn_W2).T),
        ("b2", L1_gnn_b2),
        ("wqT", np.asarray(L2_gnn_Wq).T), ("bq", columns(L2_gnn_bq)),
        ("wkT", np.asarray(L2_gnn_Wk).T), ("bk", columns(L2_gnn_bk)),
        ("wvT", np.asarray(L2_gnn_Wv).T), ("bv", L2_gnn_bv), ("woT", np.asarray(L2_gnn_Wo).T), ("bo", L2_gnn_bo),
        ("w3", L3_gnn_W), ("b3", L3_gnn_b),
    ]
    arrays, args = {}, []
    for name, a in laid_out:
        arrays[f"in_{name}"] = np.ascontiguousarray(a)
        args.append(nc.dram_tensor(f"in_{name}", arrays[f"in_{name}"].shape, F32, kind="ExternalInput").ap())
    out = nc.dram_tensor("out_x", np.asarray(x).shape, F32, kind="ExternalOutput").ap()
    gnn_stack(nc, *args, out)
    result = run_bass_kernel_spmd(nc, [arrays], core_ids=[0])
    return result.results[0]["out_x"]
```
